# Optimizing a Trainium2 kernel written in Bass

```python
import numpy as np
import jax
import jax.numpy as jnp

def _softmax(x, axis=-1):
    return jax.nn.softmax(x, axis=axis)

def _gelu(x):
    return jax.nn.gelu(x, approximate=True)

def _silu(x):
    return jax.nn.silu(x)

def _sigmoid(x):
    return jax.nn.sigmoid(x)

def _layernorm(x, axis=-1, eps=1e-05):
    m = jnp.mean(x, axis=axis, keepdims=True)
    v = jnp.var(x, axis=axis, keepdims=True)
    return (x - m) / jnp.sqrt(v + eps)

def _scatter_add(tgt, idx, src, axis=0):
    return tgt.at[idx].add(src)

def _segment_sum(src, seg, n):
    return jax.ops.segment_sum(src, seg, n)
kernel_name = 'mk_conv_preact_d1_conv_nchw64_r2_b7154a'

def setup_inputs(seed: int=0):
    np.random.seed(seed)
    _w = jnp.asarray

    def _rec_inputs():
        import jax
        import jax.numpy as jnp
        _gk = jax.random.key(seed)
        x = -7.109e-05 + 0.9999 * jax.random.normal(jax.random.fold_in(_gk, 1), (16, 32, 128, 128), jnp.float32)
        return x
    x = _rec_inputs()

    def _L0_conv_setup():
        import jax, jax.numpy as jnp
        from jax import lax
        import numpy as np
        B, C, H, W = (16, 32, 128, 128)
        K = 3
        PAD = (K - 1) // 2
        key = jax.random.key(seed)
        ks = jax.random.split(key, 5)
        x = jax.random.normal(ks[0], (B, C, H, W), dtype=jnp.float32)
        w1 = jax.random.normal(ks[1], (C * K * K, C), dtype=jnp.float32) * 0.1
        b1 = jax.random.normal(ks[2], (C * K * K,), dtype=jnp.float32) * 0.1
        fscale = jax.random.normal(ks[3], (C,), dtype=jnp.float32) * 0.1
        conv_bias = jax.random.normal(ks[4], (C,), dtype=jnp.float32) * 0.1
        return {'x': x, 'w1': w1, 'b1': b1, 'fscale': fscale, 'conv_bias': conv_bias}
    _L0_conv_all = _L0_conv_setup()
    _L0_conv_in = {k: v for k, v in _L0_conv_all.items() if k in ('w1', 'b1', 'fscale', 'conv_bias')}
    del _L0_conv_all
    return {'x': x, 'L0_conv_w1': _L0_conv_in['w1'], 'L0_conv_b1': _L0_conv_in['b1'], 'L0_conv_fscale': _L0_conv_in['fscale'], 'L0_conv_conv_bias': _L0_conv_in['conv_bias']}

def reference(x, L0_conv_w1, L0_conv_b1, L0_conv_fscale, L0_conv_conv_bias):
    import jax
    import jax.numpy as jnp

    def _L0_conv_ref(x, w1, b1, fscale, conv_bias):
        import jax, jax.numpy as jnp
        from jax import lax
        import numpy as np
        B, C, H, W = (16, 32, 128, 128)
        K = 3
        PAD = (K - 1) // 2
        b, c, h, w = x.shape
        avg = x.mean(axis=(2, 3))
        dyn = avg @ w1.T + b1
        wk = jax.nn.sigmoid(dyn).reshape(b * c, 1, K, K)
        xf = x.reshape(1, b * c, h, w)
        y = lax.conv_general_dilated(xf, wk, window_strides=(1, 1), padding=[(PAD, PAD), (PAD, PAD)], feature_group_count=b * c, dimension_numbers=('NCHW', 'OIHW', 'NCHW'))
        y = y.reshape(b, c, h, w) + conv_bias[None, :, None, None]
        fs = fscale[None, :, None, None]
        return (x - y) * fs * x + y

    def _gn(v, G=32, eps=1e-05):
        B_, C_, H_, W_ = v.shape
        g = v.reshape(B_, G, C_ // G, H_, W_)
        m = jnp.mean(g, axis=(2, 3, 4), keepdims=True)
        s = jnp.var(g, axis=(2, 3, 4), keepdims=True)
        return ((g - m) / jnp.sqrt(s + eps)).reshape(v.shape)

    def _ln_c(v, eps=1e-06):
        m = jnp.mean(v, axis=1, keepdims=True)
        s = jnp.var(v, axis=1, keepdims=True)
        return (v - m) / jnp.sqrt(s + eps)

    def _ln_t(v, eps=1e-05):
        m = jnp.mean(v, axis=-1, keepdims=True)
        s = jnp.var(v, axis=-1, keepdims=True)
        return (v - m) / jnp.sqrt(s + eps)

    def _to_tokens(v):
        B_, C_, H_, W_ = v.shape
        return v.reshape(B_, C_, H_ * W_).transpose(0, 2, 1)

    def _from_tokens(t, like):
        B_, C_, H_, W_ = like.shape
        return t.transpose(0, 2, 1).reshape(B_, C_, H_, W_)
    x = x + _L0_conv_ref(_gn(x), L0_conv_w1, L0_conv_b1, L0_conv_fscale, L0_conv_conv_bias)
    return x

_drawn_inputs = setup_inputs


def setup_inputs(seed=0):
    import zlib

    import numpy as np

    out = dict(_drawn_inputs(seed))
    spreads = {}
    factors = {}
    for name, (base, spread) in spreads.items():
        noise = np.random.default_rng([zlib.crc32(name.encode()), seed]).standard_normal(out[name].shape)
        drawn = base * np.exp(spread * noise) if base else spread * noise
        out[name] = jnp.asarray(drawn.astype(out[name].dtype))
    for name, factor in factors.items():
        out[name] = (out[name] * factor).astype(out[name].dtype)
    return out
```

```python
from contextlib import ExitStack

import numpy as np

import concourse.bass as bass
from concourse import mybir

F32 = mybir.dt.float32
F16 = mybir.dt.float16
ALU = mybir.AluOpType
ACT = mybir.ActivationFunctionType
AX_X = mybir.AxisListType.X

B, C, H, W = 16, 32, 128, 128
TAPS = 3
ROWS, HALO, SLOTS = 16, 2, 7
BLOCKS = H // ROWS
GROUPS = -(-C // SLOTS)
BODY = ROWS * SLOTS
PARTS = BODY + HALO * SLOTS
OUTS = BODY + SLOTS
LAST_SLOT = ROWS * (SLOTS - 1)
CHANS = SLOTS * GROUPS
FULL = C - GROUPS * (SLOTS - 1)
SPAN = BLOCKS * W
HALF = SPAN // 2
PADDED = W + 2
IMAGE = H * W
EPS = 1e-5
TAP_SCALE = 64.0
VARIANTS = 2 * TAPS
TAP_COLS = -(-OUTS // TAPS) * TAPS
SETS = TAPS * TAPS
EVEN, ODD = list(range(0, GROUPS, 2)), list(range(1, GROUPS, 2))
TAPS_BY = [(EVEN, ODD)[g % 2] for g in range(GROUPS)]
XBUFS = 4
LAPS = (B - XBUFS) // XBUFS

LOADS = SLOTS + HALO + 1
STORES = SLOTS + GROUPS + 2

_AT = {}
_N = 0
for _name, _width in (("average", PARTS), ("band", TAP_COLS), ("centre", GROUPS * SETS), ("spread", TAPS * CHANS),
                      ("phase", PARTS), ("own", SLOTS)):
    _AT[_name] = (_N, _N + _width)
    _N += _width
CONST_COLS = _N


def place():
    p = np.arange(PARTS)
    slot = np.where(p < BODY, p // ROWS, (p - BODY) % SLOTS)
    row = np.where(p < BODY, p % ROWS, ROWS + (p - BODY) // SLOTS)
    return slot, row


def constants():
    slot, row = place()
    own = slot[:, None] == np.arange(SLOTS)[None, :]
    same = slot[:, None] == slot[None, :]
    body = (np.arange(PARTS) < BODY)[:, None]
    near = np.abs(row[:, None] - row[None, :]) <= 1
    phase = (slot + row) % TAPS
    c = np.zeros((PARTS, CONST_COLS), np.float32)

    def put(name, value):
        a, b = _AT[name]
        c[:value.shape[0], a:b] = value.reshape(value.shape[0], -1)

    put("average", (same & body) / np.float32(ROWS))
    band = np.zeros((PARTS, TAP_COLS), np.float32)
    band[:, :OUTS] = (same & near)[:, :OUTS]
    put("band", band)
    centre = np.zeros((PARTS, GROUPS, TAPS, TAPS), np.float32)
    for p in range(PARTS):
        centre[p, :, 1, phase[p]] = -1.0
    put("centre", centre)
    spread = np.zeros((PARTS, TAPS, SLOTS, GROUPS), np.float32)
    spread[:, :, :, :] = (own & (row == 0)[:, None])[:, None, :, None]
    put("spread", spread)
    ph = np.zeros((TAPS * CHANS, PARTS), np.float32)
    for q in range(TAPS):
        ph[q * CHANS:(q + 1) * CHANS] = phase[None, :] == q
    put("phase", ph)
    put("own", own.astype(np.float32))
    return c


def lay_out(w1, b1, fscale, conv_bias):
    slot, row = place()
    phase = (slot + row) % TAPS
    w = np.zeros((CHANS, TAPS, TAPS, CHANS), np.float32)
    w[:C, :, :, :C] = w1.reshape(C, TAPS, TAPS, C)
    w = w.reshape(SLOTS, GROUPS, TAPS, TAPS, CHANS)
    b = np.zeros((CHANS, TAPS, TAPS), np.float32)
    b[:C] = b1.reshape(C, TAPS, TAPS)
    b = b.reshape(SLOTS, GROUPS, TAPS, TAPS)
    wr = np.zeros((TAPS, CHANS, GROUPS, TAPS, TAPS, SLOTS), np.float32)
    br = np.zeros((PARTS, GROUPS, TAPS, TAPS), np.float32)
    for q in range(TAPS):
        for ph in range(TAPS):
            tap = (ph - q + 1) % TAPS
            wr[ph, :, :, :, q, :] = w[:, :, tap].transpose(3, 1, 2, 0)
            mine = phase == ph
            br[mine, :, :, q] = b[slot[mine], :, tap, :]
    gate = np.zeros((2, CHANS), np.float32)
    gate[0, :C] = fscale
    gate[1, :C] = conv_bias
    gate = gate.reshape(2, SLOTS, GROUPS)[:, slot].transpose(1, 0, 2)
    return (wr.reshape(TAPS * CHANS, -1), br.reshape(PARTS, -1), np.ascontiguousarray(gate.reshape(PARTS, -1)))


def build(nc, x, w1r, b1r, gate, const, out):
    with ExitStack() as ctx:
        def sb(name, shape, dt=F32):
            return ctx.enter_context(nc.sbuf_tensor(name, shape, dt))

        def ps(name, shape):
            return ctx.enter_context(nc.psum_tensor(name, shape, F32))

        def sem(name):
            return ctx.enter_context(nc.semaphore(name))

        cst = sb("cst", [PARTS, CONST_COLS])
        w1s = sb("w1s", [TAPS * CHANS, GROUPS * SETS * SLOTS])
        b1s = sb("b1s", [PARTS, GROUPS * SETS])
        gates = sb("gates", [PARTS, 2, GROUPS])
        band = sb("band", [PARTS, TAP_COLS], F16)
        ones = sb("ones", [PARTS, PARTS])
        numbers = sb("numbers", [PARTS, 4, GROUPS])
        minus_half, eps, inv_scale, tap_scale = (numbers[:, k] for k in range(4))
        neg_fs = sb("neg_fs", [PARTS, GROUPS])
        bias64 = sb("bias64", [PARTS, GROUPS])

        def const_of(name, parts=PARTS):
            a, b = _AT[name]
            return cst[0:parts, a:b]

        xs = sb("xs", [PARTS, XBUFS, GROUPS, SPAN])
        z_hi = sb("z_hi", [PARTS, 2, GROUPS, BLOCKS, PADDED], F16)
        z_lo = sb("z_lo", [PARTS, 2, GROUPS, BLOCKS, PADDED], F16)
        taps = sb("taps", [PARTS, 2, GROUPS, VARIANTS, 128], F16)
        gate_t = sb("gate_t", [PARTS, 2, SPAN])
        gated = sb("gated", [PARTS, 2, SPAN])

        halves = sb("halves", [PARTS, GROUPS, 2, 6])
        row_stats = sb("row_stats", [PARTS, GROUPS, 2])
        neg_mean = sb("neg_mean", [PARTS, 2, GROUPS])
        moments = sb("moments", [PARTS, 2, GROUPS])
        square = sb("square", [PARTS, GROUPS])
        zstats = sb("zstats", [PARTS, 2, GROUPS])
        var_eps = sb("var_eps", [PARTS, GROUPS])
        rstd = sb("rstd", [PARTS, XBUFS, GROUPS])
        rstd64 = sb("rstd64", [PARTS, GROUPS])
        gate_scale = sb("gate_scale", [PARTS, XBUFS, GROUPS])
        gate_part = sb("gate_part", [PARTS, GROUPS])
        gate_bias = sb("gate_bias", [PARTS, XBUFS, GROUPS])
        skip_scale = sb("skip_scale", [PARTS, XBUFS, GROUPS])
        skip_bias = sb("skip_bias", [PARTS, XBUFS, GROUPS])
        avg = sb("avg", [PARTS, GROUPS])
        avg_cols = sb("avg_cols", [PARTS, TAPS * CHANS])
        avg_rows = sb("avg_rows", [TAPS * CHANS, PARTS])
        own_dyn = sb("own_dyn", [PARTS, GROUPS * SETS, SLOTS])
        dyn_sum = sb("dyn_sum", [PARTS, GROUPS * SETS])
        dyn = sb("dyn", [PARTS, GROUPS * SETS])
        sig = sb("sig", [PARTS, GROUPS * SETS])
        less_one = sb("less_one", [PARTS, GROUPS * SETS])
        tap = sb("tap", [PARTS, GROUPS, SETS])
        tap_split = sb("tap_split", [PARTS, 2, GROUPS, 2, SETS], F16)

        conv_ps = ps("conv_ps", [128, 2, 2, 512])
        stat_ps = ps("stat_ps", [128, 512])
        avg_ps = ps("avg_ps", [128, 512])
        dyn_ps = ps("dyn_ps", [128, 512])

        x_loaded = [sem(f"x_loaded{i}") for i in range(XBUFS)]
        x_stored = [sem(f"x_stored{i}") for i in range(XBUFS)]
        params_loaded = sem("params_loaded")
        consts_loaded = sem("consts_loaded")
        slots_zeroed = sem("slots_zeroed")
        pads_zeroed = sem("pads_zeroed")
        ones_set = sem("ones_set")
        gate_params_set = sem("gate_params_set")
        band_set = sem("band_set")
        halves_done = sem("halves_done")
        rows_done = sem("rows_done")
        mean_done = sem("mean_done")
        neg_mean_ready = sem("neg_mean_ready")
        dev_ready = sem("dev_ready")
        square_ready = sem("square_ready")
        moments_ready = sem("moments_ready")
        zstats_done = sem("zstats_done")
        zstats_copied = sem("zstats_copied")
        var_eps_ready = sem("var_eps_ready")
        rstd_ready = sem("rstd_ready")
        avg_ready = sem("avg_ready")
        avg_cols_ready = sem("avg_cols_ready")
        gate_scale_ready = sem("gate_scale_ready")
        gate_part_ready = sem("gate_part_ready")
        affine_ready = sem("affine_ready")
        avg_rows_done = sem("avg_rows_done")
        avg_rows_ready = sem("avg_rows_ready")
        dyn_done = sem("dyn_done")
        own_dyn_ready = sem("own_dyn_ready")
        dyn_sum_ready = sem("dyn_sum_ready")
        dyn_ready = sem("dyn_ready")
        sig_ready = sem("sig_ready")
        less_one_ready = sem("less_one_ready")
        tap_ready = sem("tap_ready")
        tap_hi_ready = sem("tap_hi_ready")
        tap_split_ready = sem("tap_split_ready")
        taps_ready = [sem("even_taps_ready"), sem("odd_taps_ready")]
        z_hi_ready = sem("z_hi_ready")
        z_lo_ready = sem("z_lo_ready")
        conv_done = sem("conv_done")
        gate_ready = sem("gate_ready")
        skip_ready = sem("skip_ready")
        gated_ready = sem("gated_ready")
        out_ready = sem("out_ready")

        block = ctx.enter_context(nc.Block())

        def at_least(eng, s, value):
            if not isinstance(value, int) or value > 0:
                eng.wait_ge(s, value)

        def batch(lap, v):
            return XBUFS * lap + 1 + v

        def uses(lap, v):
            return lap + (1 + v) // XBUFS + 1

        def in_batches(v_and_after, lap):
            return not isinstance(lap, int) or 0 <= XBUFS * lap + 1 + v_and_after < B

        def schedule(eng, step):
            for v in range(-XBUFS, 0):
                step(0, v)
            with eng.Fori(0, LAPS) as lap:
                for v in range(XBUFS):
                    step(lap, v)
            for v in range(B - 1 - XBUFS * LAPS):
                step(LAPS, v)

        def matrices(eng, lap, v, g):
            i, par = batch(lap, v), (1 + v) % 2
            eng.wait_ge(tap_split_ready, i + 1)
            shape = [PARTS, VARIANTS, TAP_COLS // TAPS, TAPS]
            eng.tensor_tensor(
                taps[:, par, g, :, 0:TAP_COLS].rearrange("p t (a q) -> p t a q", q=TAPS),
                band[:].rearrange("p (a q) -> p a q", q=TAPS).unsqueeze(1).to_broadcast(shape),
                tap_split[:, par, g].rearrange("p h (d q) -> p (h d) q", q=TAPS).unsqueeze(2).to_broadcast(shape),
                ALU.mult).then_inc(taps_ready[g % 2], 1)

        @block.sync
        def _(sp):
            sp.dma_start(cst[:], const).then_inc(consts_loaded, 16)
            sp.dma_start(w1s[:], w1r).then_inc(params_loaded, 16)
            sp.dma_start(b1s[:], b1r).then_inc(params_loaded, 16)
            sp.dma_start(gates[:].rearrange("p a g -> p (a g)"), gate).then_inc(params_loaded, 16)

            def dram(image, row, dims, v):
                return bass.AP(v.tensor, v.offset + image * IMAGE + row * W, dims)

            def load(lap, v):
                i, buf = batch(lap, v), (1 + v) % XBUFS
                if not isinstance(i, int) or i >= XBUFS:
                    sp.wait_ge(x_stored[buf], 16 * STORES * (uses(lap, v) - 1))
                src = x[i]
                tile = xs[:, buf, :, :].rearrange("p g (k w) -> p (g k) w", w=W)
                for c in range(SLOTS):
                    n = BLOCKS * (GROUPS if c < SLOTS - 1 else FULL)
                    if c == SLOTS - 1 and isinstance(i, int) and i < XBUFS:
                        sp.wait_ge(slots_zeroed, i + 1)
                    sp.dma_start(tile[ROWS * c:ROWS * (c + 1), 0:n, :],
                                 dram(GROUPS * c, 0, [[W, ROWS], [ROWS * W, n], [1, W]], src)).then_inc(x_loaded[buf], 16)
                for h in range(HALO):
                    p = BODY + SLOTS * h
                    n = BLOCKS * GROUPS
                    sp.dma_start(tile[p:p + SLOTS - 1, 0:n, :],
                                 dram(0, ROWS + h, [[GROUPS * IMAGE, SLOTS - 1], [ROWS * W, n], [1, W]], src)
                                 ).then_inc(x_loaded[buf], 16)
                n = BLOCKS * FULL - 1
                sp.dma_start(tile[BODY + SLOTS - 1:PARTS:SLOTS, 0:n, :],
                             dram(GROUPS * (SLOTS - 1), ROWS, [[W, HALO], [ROWS * W, n], [1, W]], src)
                             ).then_inc(x_loaded[buf], 16)

            def store(lap, v):
                i, buf = batch(lap, v), (1 + v) % XBUFS
                sp.wait_ge(out_ready, GROUPS * i + GROUPS)
                dst = out[i]
                tile = xs[:, buf, :, :].rearrange("p g (k w) -> p (g k) w", w=W)
                for c in range(SLOTS):
                    n = BLOCKS * (GROUPS if c < SLOTS - 1 else FULL)
                    sp.dma_start(dram(GROUPS * c, 1, [[W, ROWS - 1], [ROWS * W, n], [1, W]], dst),
                                 tile[ROWS * c + 1:ROWS * (c + 1), 0:n, :]).then_inc(x_stored[buf], 16)
                for g in range(GROUPS):
                    m = SLOTS if g < FULL else SLOTS - 1
                    sp.dma_start(dram(g, ROWS, [[GROUPS * IMAGE, m], [ROWS * W, BLOCKS - 1], [1, W]], dst),
                                 tile[BODY:BODY + m, BLOCKS * g:BLOCKS * (g + 1) - 1, :]).then_inc(x_stored[buf], 16)
                top = xs[:, buf, :, 0:W]
                sp.dma_start(dram(0, 0, [[GROUPS * IMAGE, SLOTS - 1], [IMAGE, GROUPS], [1, W]], dst),
                             top[0:ROWS * (SLOTS - 1):ROWS, :, :]).then_inc(x_stored[buf], 16)
                sp.dma_start(dram(GROUPS * (SLOTS - 1), 0, [[IMAGE, 1], [IMAGE, FULL], [1, W]], dst),
                             top[ROWS * (SLOTS - 1):ROWS * (SLOTS - 1) + 1, 0:FULL, :]).then_inc(x_stored[buf], 16)

            def step(lap, v):
                if in_batches(v + 3, lap):
                    load(lap, v + 3)
                if in_batches(v, lap):
                    store(lap, v)

            schedule(sp, step)
            for buf in range(XBUFS):
                sp.wait_ge(x_stored[buf], 16 * STORES * (B // XBUFS))

        @block.tensor
        def _(pe):
            pe.wait_ge(consts_loaded, 16)
            pe.wait_ge(params_loaded, 48)
            pe.wait_ge(ones_set, 1)

            def mean(lap, v):
                i = batch(lap, v)
                pe.wait_ge(rows_done, i + 1)
                nc.tensor.matmul(stat_ps[0:PARTS, 0:GROUPS], const_of("average"), row_stats[:, :, 0],
                                 start=True, stop=True).then_inc(mean_done, 1)

            def spread_stats(lap, v):
                i = batch(lap, v)
                pe.wait_ge(moments_ready, i + 1)
                nc.tensor.matmul(stat_ps[0:PARTS, 0:2 * GROUPS], const_of("average"),
                                 moments[:].rearrange("p a g -> p (a g)"), start=True, stop=True).then_inc(zstats_done, 1)

            def averages(lap, v):
                i = batch(lap, v)
                pe.wait_ge(avg_cols_ready, i + 1)
                nc.tensor.matmul(avg_ps[0:TAPS * CHANS, 0:PARTS], avg_cols[:], ones[:],
                                 start=True, stop=True).then_inc(avg_rows_done, 1)

            def dynamics(lap, v):
                i = batch(lap, v)
                pe.wait_ge(avg_rows_ready, i + 1)
                nc.tensor.matmul(dyn_ps[0:PARTS, 0:GROUPS * SETS * SLOTS], avg_rows[:], w1s[:],
                                 start=True, stop=True).then_inc(dyn_done, 1)

            def conv(lap, v, g):
                i, par = batch(lap, v), (1 + v) % 2
                n = GROUPS * i + g
                acc = conv_ps[:, (par + g) % 2]
                at_least(pe, gated_ready, n - 1)
                order = TAPS_BY[g].index(g)
                pe.wait_ge(taps_ready[g % 2], len(TAPS_BY[g]) * i + order + 1)
                pe.wait_ge(z_hi_ready, n + 1)
                pe.wait_ge(z_lo_ready, n + 1)
                products = [(half, z, dw) for half, z in ((0, z_hi), (0, z_lo), (1, z_hi)) for dw in range(TAPS)]
                for at, (half, z, dw) in enumerate(products):
                    first, last = at == 0, at == len(products) - 1
                    for bank, off, k0, k1, parts in ((0, 0, 0, 4, PARTS), (1, 0, 4, 7, PARTS), (1, 3 * W, 7, 8, BODY)):
                        mm = nc.tensor.matmul(acc[:, bank, off:off + (k1 - k0) * W],
                                              taps[0:parts, par, g, half * TAPS + dw, :],
                                              z[0:parts, par, g, k0:k1, dw:dw + W],
                                              start=first and off == 0, stop=last, skip_group_check=True)
                mm.then_inc(conv_done, 1)

            def step(lap, v):
                now, nxt, stats = in_batches(v, lap), in_batches(v + 1, lap), in_batches(v + 2, lap)
                for s in range(GROUPS):
                    if nxt and s == 0:
                        averages(lap, v + 1)
                    if nxt and s == 1:
                        dynamics(lap, v + 1)
                    if stats and s == 3:
                        mean(lap, v + 2)
                    if stats and s == 4:
                        spread_stats(lap, v + 2)
                    if now:
                        conv(lap, v, s)

            schedule(pe, step)

        @block.vector
        def _(dve):
            for buf in range(XBUFS):
                nc.vector.memset(xs[LAST_SLOT:PARTS, buf, FULL - 1:GROUPS], 0.0).then_inc(slots_zeroed, 1)
            dve.wait_ge(consts_loaded, 16)
            nc.vector.tensor_copy(band[:], const_of("band")).then_inc(band_set, 1)

            def bn(lap, v, g):
                i, buf = batch(lap, v), (1 + v) % XBUFS
                if g == 0:
                    dve.wait_ge(x_loaded[buf], 16 * LOADS * uses(lap, v))
                for h in range(2):
                    ins = nc.vector.bn_stats(halves[:, g, h, :], xs[:, buf, g, h * HALF:(h + 1) * HALF])
                ins.then_inc(halves_done, 1)

            def rows(lap, v):
                for g in range(GROUPS):
                    ins = nc.vector.bn_aggr(row_stats[:, g, :], halves[:, g].rearrange("p h s -> p (h s)"))
                ins.then_inc(rows_done, 1)

            def about_mean(lap, v):
                i, par = batch(lap, v), (1 + v) % 2
                dve.wait_ge(mean_done, i + 1)
                nc.vector.tensor_scalar(neg_mean[:, par], stat_ps[0:PARTS, 0:GROUPS], -1.0, None,
                                        ALU.mult).then_inc(neg_mean_ready, 1)
                dve.wait_ge(neg_mean_ready, i + 1)
                nc.vector.tensor_tensor(moments[:, 0], row_stats[:, :, 0], neg_mean[:, par],
                                        ALU.add).then_inc(dev_ready, 1)
                dve.wait_ge(dev_ready, i + 1)
                nc.vector.tensor_tensor(square[:], moments[:, 0], moments[:, 0], ALU.mult).then_inc(square_ready, 1)
                dve.wait_ge(square_ready, i + 1)
                nc.vector.tensor_tensor(moments[:, 1], row_stats[:, :, 1], square[:], ALU.add).then_inc(moments_ready, 1)

            def avg_of_phase(lap, v):
                i = batch(lap, v)
                dve.wait_ge(avg_rows_done, i + 1)
                nc.vector.tensor_tensor(avg_rows[:], avg_ps[0:TAPS * CHANS, 0:PARTS], const_of("phase", TAPS * CHANS),
                                        ALU.mult).then_inc(avg_rows_ready, 1)

            def own_taps(lap, v):
                i = batch(lap, v)
                dve.wait_ge(dyn_done, i + 1)
                nc.vector.tensor_tensor(own_dyn[:], dyn_ps[0:PARTS, 0:GROUPS * SETS * SLOTS].rearrange("p (a c) -> p a c", c=SLOTS),
                                        const_of("own").unsqueeze(1).to_broadcast([PARTS, GROUPS * SETS, SLOTS]),
                                        ALU.mult).then_inc(own_dyn_ready, 1)
                dve.wait_ge(own_dyn_ready, i + 1)
                nc.vector.tensor_reduce(dyn_sum[:], own_dyn[:], AX_X, ALU.add).then_inc(dyn_sum_ready, 1)
                dve.wait_ge(dyn_sum_ready, i + 1)
                nc.vector.tensor_tensor(dyn[:], dyn_sum[:], b1s[:], ALU.add).then_inc(dyn_ready, 1)

            def low(lap, v, g):
                i, par, buf = batch(lap, v), (1 + v) % 2, (1 + v) % XBUFS
                n = GROUPS * i + g
                at_least(dve, conv_done, n + 1 - 2 * GROUPS)
                dve.wait_ge(z_hi_ready, n + 1)
                nc.vector.scalar_tensor_tensor(
                    out=z_lo[:, par, g, :, 1:W + 1], in0=xs[:, buf, g].rearrange("p (k w) -> p k w", w=W),
                    scalar=neg_mean[:, par, g:g + 1], in1=z_hi[:, par, g, :, 1:W + 1],
                    op0=ALU.add, op1=ALU.subtract).then_inc(z_lo_ready, 1)

            def gate_conv(lap, v, g):
                i, par = batch(lap, v), (1 + v) % 2
                n, odd = GROUPS * i + g, ((1 + v) % 2 + g) % 2
                dve.wait_ge(gate_ready, n + 1)
                at_least(dve, out_ready, n - 1)
                dve.wait_ge(conv_done, n + 1)
                nc.vector.scalar_tensor_tensor(
                    out=gated[0:OUTS, odd].rearrange("p (h n) -> p h n", h=2), in0=conv_ps[0:OUTS, odd],
                    scalar=bias64[0:OUTS, g:g + 1], in1=gate_t[0:OUTS, odd].rearrange("p (h n) -> p h n", h=2),
                    op0=ALU.add, op1=ALU.mult).then_inc(gated_ready, 1)

            def step(lap, v):
                now, nxt, stats = in_batches(v, lap), in_batches(v + 1, lap), in_batches(v + 2, lap)
                for s in range(GROUPS):
                    if nxt and s == 0:
                        avg_of_phase(lap, v + 1)
                    if nxt and s == 1:
                        own_taps(lap, v + 1)
                    if stats and s == 3:
                        about_mean(lap, v + 2)
                    if stats:
                        for g in ((0, 1), (2,), (3, 4), (), ())[s]:
                            bn(lap, v + 2, g)
                    if stats and s == 2:
                        dve.wait_ge(halves_done, GROUPS * (batch(lap, v + 2) + 1))
                    if nxt:
                        low(lap, v + 1, s)
                    if stats and s == 2:
                        rows(lap, v + 2)
                    if nxt and s >= 3:
                        matrices(nc.vector, lap, v + 1, ODD[s - 3])
                    if now:
                        gate_conv(lap, v, s)

            dve.wait_ge(gate_params_set, 2)
            dve.wait_ge(params_loaded, 48)
            dve.wait_ge(slots_zeroed, XBUFS)
            dve.wait_ge(pads_zeroed, 6)
            schedule(dve, step)

        @block.scalar
        def _(act):
            act.wait_ge(pads_zeroed, 6)
            act.wait_ge(gate_params_set, 2)

            def high(lap, v, g):
                i, par, buf = batch(lap, v), (1 + v) % 2, (1 + v) % XBUFS
                n = GROUPS * i + g
                if g == 0:
                    act.wait_ge(neg_mean_ready, i + 1)
                at_least(act, conv_done, n + 1 - 2 * GROUPS)
                nc.scalar.activation(z_hi[:, par, g, :, 1:W + 1], xs[:, buf, g].rearrange("p (k w) -> p k w", w=W),
                                     ACT.Identity, bias=neg_mean[:, par, g:g + 1]).then_inc(z_hi_ready, 1)

            def gate_and_skip(lap, v, g):
                i, buf = batch(lap, v), (1 + v) % XBUFS
                n, odd = GROUPS * i + g, ((1 + v) % 2 + g) % 2
                if g == 0:
                    act.wait_ge(affine_ready, 3 * (i + 1))
                at_least(act, gated_ready, n - 1)
                nc.scalar.activation(gate_t[:, odd], xs[:, buf, g], ACT.Identity, bias=gate_bias[:, buf, g:g + 1],
                                     scale=gate_scale[:, buf, g:g + 1]).then_inc(gate_ready, 1)
                act.wait_ge(z_lo_ready, n + 1)
                nc.scalar.activation(xs[:, buf, g], xs[:, buf, g], ACT.Identity, bias=skip_bias[:, buf, g:g + 1],
                                     scale=skip_scale[:, buf, g:g + 1]).then_inc(skip_ready, 1)

            def step(lap, v):
                now, nxt, stats = in_batches(v, lap), in_batches(v + 1, lap), in_batches(v + 2, lap)
                for s in range(GROUPS):
                    if nxt:
                        high(lap, v + 1, s)
                    if stats and s == 4:
                        act.wait_ge(zstats_done, batch(lap, v + 2) + 1)
                        nc.scalar.copy(zstats[:].rearrange("p a g -> p (a g)"),
                                       stat_ps[0:PARTS, 0:2 * GROUPS]).then_inc(zstats_copied, 1)
                    if now:
                        gate_and_skip(lap, v, s)
                    if nxt and s == 1:
                        act.wait_ge(dyn_ready, batch(lap, v + 1) + 1)
                        nc.scalar.activation(sig[:], dyn[:], ACT.Sigmoid).then_inc(sig_ready, 1)

            schedule(act, step)

        @block.gpsimd
        def _(pool):
            for par in range(2):
                for z in (z_hi, z_lo):
                    nc.gpsimd.memset(z[:, par, :, :, 0:PADDED:W + 1].rearrange("p g k e -> p (g k) e"), 0.0).then_inc(pads_zeroed, 1)
                nc.gpsimd.memset(taps[:, par, :, :, TAP_COLS:].rearrange("p g t c -> p (g t) c"), 0.0).then_inc(pads_zeroed, 1)
            nc.gpsimd.memset(ones[:], 1.0).then_inc(ones_set, 1)
            for tile, number in ((minus_half, -0.5), (eps, EPS), (inv_scale, 1.0 / TAP_SCALE), (tap_scale, TAP_SCALE)):
                nc.gpsimd.memset(tile, number).then_inc(ones_set, 1)
            pool.wait_ge(params_loaded, 48)
            nc.gpsimd.tensor_scalar(neg_fs[:], gates[:, 0], -1.0 / TAP_SCALE, 0.0, ALU.mult, ALU.add).then_inc(gate_params_set, 1)
            nc.gpsimd.tensor_scalar(bias64[:], gates[:, 1], TAP_SCALE, 0.0, ALU.mult, ALU.add).then_inc(gate_params_set, 1)
            pool.wait_ge(consts_loaded, 16)
            pool.wait_ge(ones_set, 5)
            pool.wait_ge(gate_params_set, 2)
            pool.wait_ge(band_set, 1)

            def scales(lap, v):
                i, par, buf = batch(lap, v), (1 + v) % 2, (1 + v) % XBUFS
                pool.wait_ge(zstats_copied, i + 1)
                nc.gpsimd.tensor_tensor(var_eps[:], zstats[:, 1], eps, ALU.add).then_inc(var_eps_ready, 1)
                pool.wait_ge(var_eps_ready, i + 1)
                nc.gpsimd.tensor_tensor(rstd[:, buf], var_eps[:], minus_half, ALU.pow).then_inc(rstd_ready, 1)
                pool.wait_ge(rstd_ready, i + 1)
                nc.gpsimd.tensor_tensor(avg[:], zstats[:, 0], rstd[:, buf], ALU.mult).then_inc(avg_ready, 1)
                nc.gpsimd.tensor_tensor(gate_scale[:, buf], neg_fs[:], rstd[:, buf], ALU.mult).then_inc(gate_scale_ready, 1)
                pool.wait_ge(avg_ready, i + 1)
                nc.gpsimd.tensor_tensor(avg_cols[:].rearrange("p (a g) -> p a g", g=GROUPS),
                                        const_of("spread").rearrange("p (a g) -> p a g", g=GROUPS),
                                        avg[:].unsqueeze(1).to_broadcast([PARTS, TAPS * SLOTS, GROUPS]),
                                        ALU.mult).then_inc(avg_cols_ready, 1)
                pool.wait_ge(gate_scale_ready, i + 1)
                pool.wait_ge(neg_mean_ready, i + 1)
                nc.gpsimd.tensor_tensor(gate_part[:], gate_scale[:, buf], neg_mean[:, par], ALU.mult).then_inc(gate_part_ready, 1)
                nc.gpsimd.tensor_tensor(skip_bias[:, buf], rstd[:, buf], neg_mean[:, par], ALU.mult).then_inc(affine_ready, 1)
                nc.gpsimd.tensor_scalar(skip_scale[:, buf], rstd[:, buf], 1.0, 0.0, ALU.add, ALU.add).then_inc(affine_ready, 1)
                pool.wait_ge(gate_part_ready, i + 1)
                nc.gpsimd.tensor_tensor(gate_bias[:, buf], gate_part[:], inv_scale, ALU.add).then_inc(affine_ready, 1)

            def split_taps(lap, v):
                i, par, buf = batch(lap, v), (1 + v) % 2, (1 + v) % XBUFS
                pool.wait_ge(rstd_ready, i + 1)
                nc.gpsimd.tensor_tensor(rstd64[:], rstd[:, buf], tap_scale, ALU.mult).then_inc(less_one_ready, 1)
                pool.wait_ge(sig_ready, i + 1)
                nc.gpsimd.tensor_tensor(less_one[:], sig[:], const_of("centre"), ALU.add).then_inc(less_one_ready, 1)
                pool.wait_ge(less_one_ready, 2 * (i + 1))
                nc.gpsimd.tensor_tensor(tap[:], less_one[:].rearrange("p (g t) -> p g t", g=GROUPS),
                                        rstd64[:].unsqueeze(2).to_broadcast([PARTS, GROUPS, SETS]), ALU.mult).then_inc(tap_ready, 1)
                pool.wait_ge(tap_ready, i + 1)
                nc.gpsimd.tensor_tensor(tap_split[:, par, :, 0, :], tap[:], ones[:, 0:GROUPS * SETS].rearrange("p (g t) -> p g t", g=GROUPS),
                                        ALU.mult).then_inc(tap_hi_ready, 1)
                pool.wait_ge(tap_hi_ready, i + 1)
                nc.gpsimd.tensor_tensor(tap_split[:, par, :, 1, :], tap[:], tap_split[:, par, :, 0, :],
                                        ALU.subtract).then_inc(tap_split_ready, 1)

            def add_skip(lap, v, g):
                i, buf = batch(lap, v), (1 + v) % XBUFS
                n, odd = GROUPS * i + g, ((1 + v) % 2 + g) % 2
                pool.wait_ge(skip_ready, n + 1)
                pool.wait_ge(gated_ready, n + 1)
                nc.gpsimd.tensor_tensor(xs[0:OUTS, buf, g], xs[0:OUTS, buf, g], gated[0:OUTS, odd],
                                        ALU.add).then_inc(out_ready, 1)

            def step(lap, v):
                now, nxt, stats = in_batches(v, lap), in_batches(v + 1, lap), in_batches(v + 2, lap)
                for s in range(GROUPS):
                    if now and s < 2:
                        matrices(nc.gpsimd, lap, v, EVEN[1 + s])
                    if nxt and s == 2:
                        split_taps(lap, v + 1)
                    if nxt and s == 3:
                        matrices(nc.gpsimd, lap, v + 1, EVEN[0])
                    if stats and s == 4:
                        scales(lap, v + 2)
                    if now:
                        add_skip(lap, v, s)

            schedule(pool, step)


def kernel(x, L0_conv_w1, L0_conv_b1, L0_conv_fscale, L0_conv_conv_bias):
    from concourse import bacc
    from concourse.bass_utils import run_bass_kernel_spmd

    w1r, b1r, gate = lay_out(np.asarray(L0_conv_w1), np.asarray(L0_conv_b1), np.asarray(L0_conv_fscale),
                             np.asarray(L0_conv_conv_bias))
    arrays = {"x": np.ascontiguousarray(x), "w1r": w1r, "b1r": b1r, "gate": gate, "const": constants()}
    nc = bacc.Bacc("TRN2", target_bir_lowering=False, num_devices=1)
    ins = [nc.dram_tensor(n, a.shape, mybir.dt.from_np(a.dtype), kind="ExternalInput").ap() for n, a in arrays.items()]
    out = nc.dram_tensor("out", (B, C, H, W), F32, kind="ExternalOutput").ap()
    build(nc, *ins, out)
    return run_bass_kernel_spmd(nc, [arrays], core_ids=[0]).results[0]["out"]
```

```python
from contextlib import ExitStack

import numpy as np

import concourse.bass as bass
from concourse import mybir

F32 = mybir.dt.float32
F16 = mybir.dt.float16
ALU = mybir.AluOpType
ACT = mybir.ActivationFunctionType
AX_X = mybir.AxisListType.X

B, C, H, W = 16, 32, 128, 128
TAPS = 3
ROWS, SLOTS = 16, 8
PARTS = ROWS * SLOTS
GROUPS = C // SLOTS
STEP = ROWS - 2
BLOCKS = (H - 2) // STEP
SPAN = BLOCKS * W
BANKS = 3
PER_BANK = BLOCKS // BANKS
PIECES = ((0, 1), (1, 5), (5, 9))
PADDED = W + 2
IMAGE = H * W
EPS = 1e-5
TAP_SCALE = 64.0
VARIANTS = 2 * TAPS
TAP_COLS = -(-PARTS // TAPS) * TAPS
MATRIX = 132
SETS = TAPS * TAPS
BY_VECTOR, BY_POOL = (0, 1), (2, 3)
XBUFS = 4
LAPS = (B - XBUFS) // XBUFS

LOADS = BLOCKS
STORES = BLOCKS + 2

_AT = {}
_N = 0
for _name, _width in (("average", PARTS), ("band", TAP_COLS), ("centre", GROUPS * SETS), ("spread", TAPS * C),
                      ("phase", PARTS), ("own", SLOTS), ("counts", GROUPS * 2 * 6)):
    _AT[_name] = (_N, _N + _width)
    _N += _width
CONST_COLS = _N


def place():
    p = np.arange(PARTS)
    return p % SLOTS, p // SLOTS


def constants():
    slot, row = place()
    own = slot[:, None] == np.arange(SLOTS)[None, :]
    same = slot[:, None] == slot[None, :]
    near = np.abs(row[:, None] - row[None, :]) <= 1
    phase = np.arange(PARTS) % TAPS
    c = np.zeros((PARTS, CONST_COLS), np.float32)

    def put(name, value):
        a, b = _AT[name]
        c[:value.shape[0], a:b] = value.reshape(value.shape[0], -1)

    new = np.where(row < ROWS - STEP, W, SPAN).astype(np.float32) / np.float32(IMAGE)
    put("average", same * new[:, None])
    counts = np.ones((PARTS, GROUPS, 2, 6), np.float32)
    counts[row < ROWS - STEP] = 0.0
    put("counts", counts)
    band = np.zeros((PARTS, TAP_COLS), np.float32)
    band[:, :PARTS] = same & near
    put("band", band)
    centre = np.zeros((PARTS, GROUPS, TAPS, TAPS), np.float32)
    for p in range(PARTS):
        centre[p, :, 1, phase[p]] = -1.0
    put("centre", centre)
    spread = np.zeros((PARTS, TAPS, SLOTS, GROUPS), np.float32)
    spread[:, :, :, :] = (own & (row == 0)[:, None])[:, None, :, None]
    put("spread", spread)
    ph = np.zeros((TAPS * C, PARTS), np.float32)
    for q in range(TAPS):
        ph[q * C:(q + 1) * C] = phase[None, :] == q
    put("phase", ph)
    put("own", own.astype(np.float32))
    return c


def lay_out(w1, b1, fscale, conv_bias):
    slot, row = place()
    phase = np.arange(PARTS) % TAPS
    w = w1.reshape(SLOTS, GROUPS, TAPS, TAPS, SLOTS, GROUPS)
    b = b1.reshape(SLOTS, GROUPS, TAPS, TAPS)
    wr = np.zeros((TAPS, SLOTS, GROUPS, GROUPS, TAPS, TAPS, SLOTS), np.float32)
    br = np.zeros((PARTS, GROUPS, TAPS, TAPS), np.float32)
    for q in range(TAPS):
        for ph in range(TAPS):
            tap = (q - ph + 1) % TAPS
            wr[ph, :, :, :, :, q, :] = w[:, :, tap].transpose(3, 4, 1, 2, 0)
            mine = phase == ph
            br[mine, :, :, q] = b[slot[mine], :, tap, :]
    gate = np.stack([fscale.reshape(SLOTS, GROUPS)[slot], conv_bias.reshape(SLOTS, GROUPS)[slot]], axis=1)
    return (wr.reshape(TAPS * C, -1), br.reshape(PARTS, -1), np.ascontiguousarray(gate.reshape(PARTS, -1)))


def build(nc, x, w1r, b1r, gate, const, out):
    with ExitStack() as ctx:
        def sb(name, shape, dt=F32):
            return ctx.enter_context(nc.sbuf_tensor(name, shape, dt))

        def ps(name, shape):
            return ctx.enter_context(nc.psum_tensor(name, shape, F32))

        def sem(name):
            return ctx.enter_context(nc.semaphore(name))

        cst = sb("cst", [PARTS, CONST_COLS])
        w1s = sb("w1s", [TAPS * C, GROUPS * SETS * SLOTS])
        b1s = sb("b1s", [PARTS, GROUPS * SETS])
        gates = sb("gates", [PARTS, 2, GROUPS])
        band = sb("band", [PARTS, TAP_COLS], F16)
        ones = sb("ones", [PARTS, PARTS])
        numbers = sb("numbers", [PARTS, 4, GROUPS])
        minus_half, eps, inv_scale, tap_scale = (numbers[:, k] for k in range(4))
        neg_fs = sb("neg_fs", [PARTS, GROUPS])
        bias64 = sb("bias64", [PARTS, GROUPS])

        def const_of(name, parts=PARTS):
            a, b = _AT[name]
            return cst[0:parts, a:b]

        xs = sb("xs", [PARTS, XBUFS, GROUPS, SPAN])
        z_hi = sb("z_hi", [PARTS, 2, GROUPS, BLOCKS, PADDED], F16)
        z_lo = sb("z_lo", [PARTS, 2, GROUPS, BLOCKS, PADDED], F16)
        taps = sb("taps", [PARTS, 2, GROUPS, VARIANTS, MATRIX], F16)
        outs = sb("outs", [PARTS, 2, GROUPS, SPAN])
        gated = sb("gated", [PARTS, GROUPS, SPAN])

        pieces = sb("pieces", [PARTS, GROUPS, len(PIECES), 6])
        row_stats = sb("row_stats", [PARTS, GROUPS, 2])
        neg_mean = sb("neg_mean", [PARTS, 2, GROUPS])
        moments = sb("moments", [PARTS, 2, GROUPS])
        square = sb("square", [PARTS, GROUPS])
        zstats = sb("zstats", [PARTS, 2, GROUPS])
        var_eps = sb("var_eps", [PARTS, GROUPS])
        rstd = sb("rstd", [PARTS, XBUFS, GROUPS])
        rstd64 = sb("rstd64", [PARTS, GROUPS])
        gate_scale = sb("gate_scale", [PARTS, XBUFS, GROUPS])
        gate_part = sb("gate_part", [PARTS, GROUPS])
        gate_bias = sb("gate_bias", [PARTS, XBUFS, GROUPS])
        skip_scale = sb("skip_scale", [PARTS, XBUFS, GROUPS])
        skip_bias = sb("skip_bias", [PARTS, XBUFS, GROUPS])
        avg = sb("avg", [PARTS, GROUPS])
        avg_cols = sb("avg_cols", [PARTS, TAPS * C])
        avg_rows = sb("avg_rows", [TAPS * C, PARTS])
        own_dyn = sb("own_dyn", [PARTS, GROUPS * SETS, SLOTS])
        dyn_sum = sb("dyn_sum", [PARTS, GROUPS * SETS])
        dyn = sb("dyn", [PARTS, GROUPS * SETS])
        sig = sb("sig", [PARTS, GROUPS * SETS])
        less_one = sb("less_one", [PARTS, GROUPS * SETS])
        tap = sb("tap", [PARTS, GROUPS, SETS])
        tap_split = sb("tap_split", [PARTS, 2, GROUPS, 2, SETS], F16)

        conv_ps = ps("conv_ps", [128, 2, BANKS, 512])
        stat_ps = ps("stat_ps", [128, 512])
        dyn_ps = ps("dyn_ps", [128, 512])
        mean_ps = stat_ps[:, 0:GROUPS]
        zstats_ps = stat_ps[:, GROUPS:3 * GROUPS]
        avg_ps = stat_ps[0:TAPS * C, 128:128 + PARTS]

        x_loaded = [sem(f"x_loaded{i}") for i in range(XBUFS)]
        outs_free = [sem(f"outs_free{i}") for i in range(2)]
        params_loaded = sem("params_loaded")
        consts_loaded = sem("consts_loaded")
        pads_zeroed = sem("pads_zeroed")
        ones_set = sem("ones_set")
        gate_params_set = sem("gate_params_set")
        band_set = sem("band_set")
        pieces_done = sem("pieces_done")
        counted_ready = sem("counted_ready")
        rows_done = sem("rows_done")
        mean_done = sem("mean_done")
        neg_mean_ready = sem("neg_mean_ready")
        dev_ready = sem("dev_ready")
        square_ready = sem("square_ready")
        moments_ready = sem("moments_ready")
        zstats_done = sem("zstats_done")
        zstats_copied = sem("zstats_copied")
        var_eps_ready = sem("var_eps_ready")
        rstd_ready = sem("rstd_ready")
        avg_ready = sem("avg_ready")
        avg_cols_ready = sem("avg_cols_ready")
        gate_scale_ready = sem("gate_scale_ready")
        gate_part_ready = sem("gate_part_ready")
        affine_ready = sem("affine_ready")
        avg_rows_done = sem("avg_rows_done")
        avg_rows_ready = sem("avg_rows_ready")
        dyn_done = sem("dyn_done")
        own_dyn_ready = sem("own_dyn_ready")
        dyn_sum_ready = sem("dyn_sum_ready")
        dyn_ready = sem("dyn_ready")
        sig_ready = sem("sig_ready")
        less_one_ready = sem("less_one_ready")
        tap_ready = sem("tap_ready")
        tap_hi_ready = sem("tap_hi_ready")
        tap_split_ready = sem("tap_split_ready")
        vector_taps_ready, pool_taps_ready = sem("vector_taps_ready"), sem("pool_taps_ready")
        z_hi_ready = sem("z_hi_ready")
        z_lo_ready = sem("z_lo_ready")
        conv_done = sem("conv_done")
        gate_ready = sem("gate_ready")
        skip_ready = sem("skip_ready")
        gated_ready = sem("gated_ready")
        out_ready = sem("out_ready")

        block = ctx.enter_context(nc.Block())

        def at_least(eng, s, value):
            if not isinstance(value, int) or value > 0:
                eng.wait_ge(s, value)

        def batch(lap, v):
            return XBUFS * lap + 1 + v

        def uses(lap, v):
            return lap + (1 + v) // XBUFS + 1

        def in_batches(v_and_after, lap):
            return not isinstance(lap, int) or 0 <= XBUFS * lap + 1 + v_and_after < B

        def schedule(eng, step, first=-XBUFS):
            for v in range(first, 0):
                step(0, v)
            with eng.Fori(0, LAPS) as lap:
                for v in range(XBUFS):
                    step(lap, v)
            for v in range(B - 1 - XBUFS * LAPS):
                step(LAPS, v)

        def matrices(eng, lap, v, g):
            i, par = batch(lap, v), (1 + v) % 2
            eng.wait_ge(tap_split_ready, i + 1)
            shape = [PARTS, VARIANTS, TAP_COLS // TAPS, TAPS]
            eng.tensor_tensor(
                taps[:, par, g, :, 0:TAP_COLS].rearrange("p t (a q) -> p t a q", q=TAPS),
                band[:].rearrange("p (a q) -> p a q", q=TAPS).unsqueeze(1).to_broadcast(shape),
                tap_split[:, par, g].rearrange("p h (d q) -> p (h d) q", q=TAPS).unsqueeze(2).to_broadcast(shape),
                ALU.mult).then_inc(pool_taps_ready if g in BY_POOL else vector_taps_ready, 1)

        @block.sync
        def _(sp):
            sp.dma_start(cst[:], const).then_inc(consts_loaded, 16)

            def rows_of(image, first, count):
                return bass.AP(image.tensor, image.offset + first * W, [[W, count], [IMAGE, C], [1, W]])

            def load(lap, v):
                i, buf = batch(lap, v), (1 + v) % XBUFS
                if not isinstance(i, int) or i >= XBUFS:
                    sp.wait_ge(skip_ready, GROUPS * i - GROUPS * (XBUFS - 1))
                    sp.wait_ge(z_lo_ready, GROUPS * i - GROUPS * (XBUFS - 1))
                src = x[i]
                for k in range(BLOCKS):
                    sp.dma_start(xs[:, buf, :, k * W:(k + 1) * W], rows_of(src, STEP * k, ROWS)).then_inc(x_loaded[buf], 16)

            def store(lap, v):
                i, par = batch(lap, v), (1 + v) % 2
                sp.wait_ge(out_ready, GROUPS * i + GROUPS)
                dst = out[i]
                for k in range(BLOCKS):
                    sp.dma_start(rows_of(dst, STEP * k + 1, STEP),
                                 outs[SLOTS:PARTS - SLOTS, par, :, k * W:(k + 1) * W]).then_inc(outs_free[par], 16)
                sp.dma_start(rows_of(dst, 0, 1), outs[0:SLOTS, par, :, 0:W]).then_inc(outs_free[par], 16)
                sp.dma_start(rows_of(dst, H - 1, 1), outs[PARTS - SLOTS:, par, :, SPAN - W:]).then_inc(outs_free[par], 16)

            def step(lap, v):
                if in_batches(v + 3, lap):
                    load(lap, v + 3)
                if in_batches(v - 1, lap):
                    store(lap, v - 1)

            load(0, -1)
            sp.dma_start(w1s[:], w1r).then_inc(params_loaded, 16)
            sp.dma_start(b1s[:], b1r).then_inc(params_loaded, 16)
            sp.dma_start(gates[:].rearrange("p a g -> p (a g)"), gate).then_inc(params_loaded, 16)
            schedule(sp, step, first=1 - XBUFS)
            store(LAPS, B - 2 - XBUFS * LAPS)
            for par in range(2):
                sp.wait_ge(outs_free[par], 16 + 16 * STORES * (B // 2))

        @block.tensor
        def _(pe):
            pe.wait_ge(consts_loaded, 16)
            pe.wait_ge(params_loaded, 48)
            pe.wait_ge(ones_set, 1)

            def mean(lap, v):
                i = batch(lap, v)
                pe.wait_ge(rows_done, i + 1)
                nc.tensor.matmul(mean_ps, const_of("average"), row_stats[:, :, 0],
                                 start=True, stop=True).then_inc(mean_done, 1)

            def spread_stats(lap, v):
                i = batch(lap, v)
                pe.wait_ge(moments_ready, i + 1)
                nc.tensor.matmul(zstats_ps, const_of("average"),
                                 moments[:].rearrange("p a g -> p (a g)"), start=True, stop=True).then_inc(zstats_done, 1)

            def averages(lap, v):
                i = batch(lap, v)
                pe.wait_ge(avg_cols_ready, i + 1)
                nc.tensor.matmul(avg_ps, avg_cols[:], ones[:],
                                 start=True, stop=True).then_inc(avg_rows_done, 1)

            def dynamics(lap, v):
                i = batch(lap, v)
                pe.wait_ge(avg_rows_ready, i + 1)
                nc.tensor.matmul(dyn_ps[0:PARTS, 0:GROUPS * SETS * SLOTS], avg_rows[:], w1s[:],
                                 start=True, stop=True).then_inc(dyn_done, 1)

            def conv(lap, v, g):
                i, par = batch(lap, v), (1 + v) % 2
                n = GROUPS * i + g
                acc = conv_ps[:, g % 2]
                at_least(pe, gated_ready, n - 1)
                if g in BY_POOL:
                    pe.wait_ge(pool_taps_ready, len(BY_POOL) * i + BY_POOL.index(g) + 1)
                else:
                    pe.wait_ge(vector_taps_ready, len(BY_VECTOR) * i + BY_VECTOR.index(g) + 1)
                pe.wait_ge(z_hi_ready, n + 1)
                pe.wait_ge(z_lo_ready, n + 1)
                products = [(half, z, dw) for half, z in ((0, z_hi), (0, z_lo), (1, z_hi)) for dw in range(TAPS)]
                for at, (half, z, dw) in enumerate(products):
                    first, last = at == 0, at == len(products) - 1
                    for bank in range(BANKS):
                        mm = nc.tensor.matmul(acc[:, bank, 0:PER_BANK * W], taps[:, par, g, half * TAPS + dw, 0:PARTS],
                                              z[:, par, g, PER_BANK * bank:PER_BANK * (bank + 1), dw:dw + W],
                                              start=first, stop=last)
                mm.then_inc(conv_done, 1)

            def step(lap, v):
                now, nxt, stats = in_batches(v, lap), in_batches(v + 1, lap), in_batches(v + 2, lap)
                for s in range(GROUPS):
                    if nxt and s == 0:
                        averages(lap, v + 1)
                    if nxt and s == 1:
                        dynamics(lap, v + 1)
                    if stats and s == 1:
                        mean(lap, v + 2)
                    if stats and s == 2:
                        spread_stats(lap, v + 2)
                    if now:
                        conv(lap, v, s)

            schedule(pe, step)

        @block.vector
        def _(dve):
            dve.wait_ge(consts_loaded, 16)
            nc.vector.tensor_copy(band[:], const_of("band")).then_inc(band_set, 1)

            def bn(lap, v, g):
                i, buf = batch(lap, v), (1 + v) % XBUFS
                if g == 0:
                    dve.wait_ge(x_loaded[buf], 16 * LOADS * uses(lap, v))
                for h, (a, b) in enumerate(PIECES):
                    ins = nc.vector.bn_stats(pieces[:, g, h, :], xs[:, buf, g, a * W:b * W])
                ins.then_inc(pieces_done, 1)

            def count(lap, v):
                dve.wait_ge(pieces_done, GROUPS * (batch(lap, v) + 1))
                nc.vector.tensor_tensor(pieces[:, :, 1:], pieces[:, :, 1:],
                                        const_of("counts").rearrange("p (g k e) -> p g k e", g=GROUPS, e=6),
                                        ALU.mult).then_inc(counted_ready, 1)

            def rows(lap, v):
                for g in range(GROUPS):
                    ins = nc.vector.bn_aggr(row_stats[:, g, :], pieces[:, g].rearrange("p h s -> p (h s)"))
                ins.then_inc(rows_done, 1)

            def about_mean(lap, v):
                i, par = batch(lap, v), (1 + v) % 2
                dve.wait_ge(mean_done, i + 1)
                nc.vector.tensor_scalar(neg_mean[:, par], mean_ps, -1.0, None,
                                        ALU.mult).then_inc(neg_mean_ready, 1)
                dve.wait_ge(neg_mean_ready, i + 1)
                nc.vector.tensor_tensor(moments[:, 0], row_stats[:, :, 0], neg_mean[:, par],
                                        ALU.add).then_inc(dev_ready, 1)
                dve.wait_ge(dev_ready, i + 1)
                nc.vector.tensor_tensor(square[:], moments[:, 0], moments[:, 0], ALU.mult).then_inc(square_ready, 1)
                dve.wait_ge(square_ready, i + 1)
                nc.vector.tensor_tensor(moments[:, 1], row_stats[:, :, 1], square[:], ALU.add).then_inc(moments_ready, 1)

            def copy_stats(lap, v):
                dve.wait_ge(zstats_done, batch(lap, v) + 1)
                nc.vector.tensor_copy(zstats[:].rearrange("p a g -> p (a g)"), zstats_ps).then_inc(zstats_copied, 1)

            def channel_averages(lap, v):
                i, buf = batch(lap, v), (1 + v) % XBUFS
                dve.wait_ge(rstd_ready, i + 1)
                nc.vector.tensor_tensor(avg[:], zstats[:, 0], rstd[:, buf], ALU.mult).then_inc(avg_ready, 1)
                dve.wait_ge(avg_ready, i + 1)
                nc.vector.tensor_tensor(avg_cols[:].rearrange("p (a g) -> p a g", g=GROUPS),
                                        const_of("spread").rearrange("p (a g) -> p a g", g=GROUPS),
                                        avg[:].unsqueeze(1).to_broadcast([PARTS, TAPS * SLOTS, GROUPS]),
                                        ALU.mult).then_inc(avg_cols_ready, 1)

            def avg_of_phase(lap, v):
                i = batch(lap, v)
                dve.wait_ge(avg_rows_done, i + 1)
                nc.vector.tensor_tensor(avg_rows[:], avg_ps, const_of("phase", TAPS * C),
                                        ALU.mult).then_inc(avg_rows_ready, 1)

            def own_taps(lap, v):
                i = batch(lap, v)
                dve.wait_ge(dyn_done, i + 1)
                nc.vector.tensor_tensor(own_dyn[:], dyn_ps[0:PARTS, 0:GROUPS * SETS * SLOTS].rearrange("p (a c) -> p a c", c=SLOTS),
                                        const_of("own").unsqueeze(1).to_broadcast([PARTS, GROUPS * SETS, SLOTS]),
                                        ALU.mult).then_inc(own_dyn_ready, 1)
                dve.wait_ge(own_dyn_ready, i + 1)
                nc.vector.tensor_reduce(dyn_sum[:], own_dyn[:], AX_X, ALU.add).then_inc(dyn_sum_ready, 1)
                dve.wait_ge(dyn_sum_ready, i + 1)
                nc.vector.tensor_tensor(dyn[:], dyn_sum[:], b1s[:], ALU.add).then_inc(dyn_ready, 1)

            def low(lap, v, g):
                i, par, buf = batch(lap, v), (1 + v) % 2, (1 + v) % XBUFS
                n = GROUPS * i + g
                at_least(dve, conv_done, n + 1 - 2 * GROUPS)
                dve.wait_ge(z_hi_ready, n + 1)
                nc.vector.scalar_tensor_tensor(
                    out=z_lo[:, par, g, :, 1:W + 1], in0=xs[:, buf, g].rearrange("p (k w) -> p k w", w=W),
                    scalar=neg_mean[:, par, g:g + 1], in1=z_hi[:, par, g, :, 1:W + 1],
                    op0=ALU.add, op1=ALU.subtract).then_inc(z_lo_ready, 1)

            def gate_conv(lap, v, g):
                n = GROUPS * batch(lap, v) + g
                dve.wait_ge(gate_ready, n + 1)
                dve.wait_ge(conv_done, n + 1)
                tile = gated[:, g].rearrange("p (h n) -> p h n", h=BANKS)
                nc.vector.scalar_tensor_tensor(out=tile, in0=conv_ps[:, g % 2, :, 0:PER_BANK * W], scalar=bias64[:, g:g + 1],
                                               in1=tile, op0=ALU.add, op1=ALU.mult).then_inc(gated_ready, 1)

            def step(lap, v):
                now, nxt, stats, rows_in = (in_batches(v + k, lap) for k in range(4))
                if stats:
                    rows(lap, v + 2)
                if nxt:
                    avg_of_phase(lap, v + 1)
                    low(lap, v + 1, 0)
                    low(lap, v + 1, 1)
                if now:
                    gate_conv(lap, v, 0)
                if nxt:
                    own_taps(lap, v + 1)
                if stats:
                    about_mean(lap, v + 2)
                if nxt:
                    low(lap, v + 1, 2)
                if now:
                    gate_conv(lap, v, 1)
                if stats:
                    copy_stats(lap, v + 2)
                if nxt:
                    low(lap, v + 1, 3)
                if rows_in:
                    bn(lap, v + 3, 0)
                    bn(lap, v + 3, 1)
                if now:
                    gate_conv(lap, v, 2)
                if stats:
                    channel_averages(lap, v + 2)
                if nxt:
                    for g in BY_VECTOR:
                        matrices(nc.vector, lap, v + 1, g)
                if rows_in:
                    bn(lap, v + 3, 2)
                    bn(lap, v + 3, 3)
                    count(lap, v + 3)
                    dve.wait_ge(counted_ready, batch(lap, v + 3) + 1)
                if now:
                    gate_conv(lap, v, 3)

            dve.wait_ge(gate_params_set, 2)
            dve.wait_ge(params_loaded, 48)
            dve.wait_ge(pads_zeroed, 4)
            schedule(dve, step)

        @block.scalar
        def _(act):
            act.wait_ge(pads_zeroed, 4)
            act.wait_ge(gate_params_set, 2)

            def high(lap, v, g):
                i, par, buf = batch(lap, v), (1 + v) % 2, (1 + v) % XBUFS
                n = GROUPS * i + g
                if g == 0:
                    act.wait_ge(neg_mean_ready, i + 1)
                at_least(act, conv_done, n + 1 - 2 * GROUPS)
                nc.scalar.activation(z_hi[:, par, g, :, 1:W + 1], xs[:, buf, g].rearrange("p (k w) -> p k w", w=W),
                                     ACT.Identity, bias=neg_mean[:, par, g:g + 1]).then_inc(z_hi_ready, 1)

            def gate_and_skip(lap, v, g):
                i, par, buf = batch(lap, v), (1 + v) % 2, (1 + v) % XBUFS
                n = GROUPS * i + g
                if g == 0:
                    act.wait_ge(affine_ready, 3 * (i + 1))
                at_least(act, out_ready, n + 1 - GROUPS)
                nc.scalar.activation(gated[:, g], xs[:, buf, g], ACT.Identity, bias=gate_bias[:, buf, g:g + 1],
                                     scale=gate_scale[:, buf, g:g + 1]).then_inc(gate_ready, 1)
                if g == 0:
                    act.wait_ge(outs_free[par], 16 + 16 * STORES * (XBUFS // 2 * lap + (1 + v) // 2))
                nc.scalar.activation(outs[:, par, g], xs[:, buf, g], ACT.Identity, bias=skip_bias[:, buf, g:g + 1],
                                     scale=skip_scale[:, buf, g:g + 1]).then_inc(skip_ready, 1)

            def step(lap, v):
                now, nxt = in_batches(v, lap), in_batches(v + 1, lap)
                for s in range(GROUPS):
                    if nxt:
                        high(lap, v + 1, s)
                    if now:
                        gate_and_skip(lap, v, s)
                    if nxt and s == 2:
                        act.wait_ge(dyn_ready, batch(lap, v + 1) + 1)
                        nc.scalar.activation(sig[:], dyn[:], ACT.Sigmoid).then_inc(sig_ready, 1)

            schedule(act, step)

        @block.gpsimd
        def _(pool):
            for par in range(2):
                for z in (z_hi, z_lo):
                    nc.gpsimd.memset(z[:, par, :, :, 0:PADDED:W + 1].rearrange("p g k e -> p (g k) e"), 0.0).then_inc(pads_zeroed, 1)
            for par in range(2):
                nc.gpsimd.memset(outs[:, par, 0, 0:1], 0.0).then_inc(outs_free[par], 16)
            nc.gpsimd.memset(ones[:], 1.0).then_inc(ones_set, 1)
            for tile, number in ((minus_half, -0.5), (eps, EPS), (inv_scale, 1.0 / TAP_SCALE), (tap_scale, TAP_SCALE)):
                nc.gpsimd.memset(tile, number).then_inc(ones_set, 1)
            pool.wait_ge(params_loaded, 48)
            nc.gpsimd.tensor_scalar(neg_fs[:], gates[:, 0], -1.0 / TAP_SCALE, 0.0, ALU.mult, ALU.add).then_inc(gate_params_set, 1)
            nc.gpsimd.tensor_scalar(bias64[:], gates[:, 1], TAP_SCALE, 0.0, ALU.mult, ALU.add).then_inc(gate_params_set, 1)
            pool.wait_ge(consts_loaded, 16)
            pool.wait_ge(ones_set, 5)
            pool.wait_ge(gate_params_set, 2)
            pool.wait_ge(band_set, 1)

            def inverse_deviation(lap, v):
                i, buf = batch(lap, v), (1 + v) % XBUFS
                pool.wait_ge(zstats_copied, i + 1)
                nc.gpsimd.tensor_tensor(var_eps[:], zstats[:, 1], eps, ALU.add).then_inc(var_eps_ready, 1)
                pool.wait_ge(var_eps_ready, i + 1)
                nc.gpsimd.tensor_tensor(rstd[:, buf], var_eps[:], minus_half, ALU.pow).then_inc(rstd_ready, 1)

            def factors(lap, v):
                i, par, buf = batch(lap, v), (1 + v) % 2, (1 + v) % XBUFS
                pool.wait_ge(rstd_ready, i + 1)
                nc.gpsimd.tensor_tensor(gate_scale[:, buf], neg_fs[:], rstd[:, buf], ALU.mult).then_inc(gate_scale_ready, 1)
                nc.gpsimd.tensor_tensor(skip_bias[:, buf], rstd[:, buf], neg_mean[:, par], ALU.mult).then_inc(affine_ready, 1)
                nc.gpsimd.tensor_tensor(skip_scale[:, buf], rstd[:, buf], ones[:, 0:GROUPS], ALU.add).then_inc(affine_ready, 1)
                pool.wait_ge(gate_scale_ready, i + 1)
                nc.gpsimd.tensor_tensor(gate_part[:], gate_scale[:, buf], neg_mean[:, par], ALU.mult).then_inc(gate_part_ready, 1)
                pool.wait_ge(gate_part_ready, i + 1)
                nc.gpsimd.tensor_tensor(gate_bias[:, buf], gate_part[:], inv_scale, ALU.add).then_inc(affine_ready, 1)

            def split_taps(lap, v):
                i, par, buf = batch(lap, v), (1 + v) % 2, (1 + v) % XBUFS
                pool.wait_ge(rstd_ready, i + 1)
                nc.gpsimd.tensor_tensor(rstd64[:], rstd[:, buf], tap_scale, ALU.mult).then_inc(less_one_ready, 1)
                pool.wait_ge(sig_ready, i + 1)
                nc.gpsimd.tensor_tensor(less_one[:], sig[:], const_of("centre"), ALU.add).then_inc(less_one_ready, 1)
                pool.wait_ge(less_one_ready, 2 * (i + 1))
                nc.gpsimd.tensor_tensor(tap[:], less_one[:].rearrange("p (g t) -> p g t", g=GROUPS),
                                        rstd64[:].unsqueeze(2).to_broadcast([PARTS, GROUPS, SETS]), ALU.mult).then_inc(tap_ready, 1)
                pool.wait_ge(tap_ready, i + 1)
                nc.gpsimd.tensor_tensor(tap_split[:, par, :, 0, :], tap[:], ones[:, 0:GROUPS * SETS].rearrange("p (g t) -> p g t", g=GROUPS),
                                        ALU.mult).then_inc(tap_hi_ready, 1)
                pool.wait_ge(tap_hi_ready, i + 1)
                nc.gpsimd.tensor_tensor(tap_split[:, par, :, 1, :], tap[:], tap_split[:, par, :, 0, :],
                                        ALU.subtract).then_inc(tap_split_ready, 1)

            def add_skip(lap, v, g):
                par, n = (1 + v) % 2, GROUPS * batch(lap, v) + g
                pool.wait_ge(skip_ready, n + 1)
                pool.wait_ge(gated_ready, n + 1)
                nc.gpsimd.tensor_tensor(outs[:, par, g], outs[:, par, g], gated[:, g], ALU.add).then_inc(out_ready, 1)

            def step(lap, v):
                now, nxt, stats = in_batches(v, lap), in_batches(v + 1, lap), in_batches(v + 2, lap)
                for s in range(GROUPS):
                    if now and s < len(BY_POOL):
                        matrices(nc.gpsimd, lap, v, BY_POOL[s])
                    if stats and s == 2:
                        inverse_deviation(lap, v + 2)
                    if nxt and s == 1:
                        split_taps(lap, v + 1)
                    if stats and s == 3:
                        factors(lap, v + 2)
                    if now:
                        add_skip(lap, v, s)

            schedule(pool, step)


def kernel(x, L0_conv_w1, L0_conv_b1, L0_conv_fscale, L0_conv_conv_bias):
    from concourse import bacc
    from concourse.bass_utils import run_bass_kernel_spmd

    w1r, b1r, gate = lay_out(np.asarray(L0_conv_w1), np.asarray(L0_conv_b1), np.asarray(L0_conv_fscale),
                             np.asarray(L0_conv_conv_bias))
    arrays = {"x": np.ascontiguousarray(x), "w1r": w1r, "b1r": b1r, "gate": gate, "const": constants()}
    nc = bacc.Bacc("TRN2", target_bir_lowering=False, num_devices=1)
    ins = [nc.dram_tensor(n, a.shape, mybir.dt.from_np(a.dtype), kind="ExternalInput").ap() for n, a in arrays.items()]
    out = nc.dram_tensor("out", (B, C, H, W), F32, kind="ExternalOutput").ap()
    build(nc, *ins, out)
    return run_bass_kernel_spmd(nc, [arrays], core_ids=[0]).results[0]["out"]
```

```python
from contextlib import ExitStack

import numpy as np

import concourse.bass as bass
from concourse import mybir

F32 = mybir.dt.float32
F16 = mybir.dt.float16
ALU = mybir.AluOpType
ACT = mybir.ActivationFunctionType
AX_X = mybir.AxisListType.X

B, C, H, W = 16, 32, 128, 128
TAPS = 3
ROWS, SLOTS = 16, 8
PARTS = ROWS * SLOTS
GROUPS = C // SLOTS
STEP = ROWS - 2
BLOCKS = (H - 2) // STEP
SPAN = BLOCKS * W
BANKS = 3
PER_BANK = BLOCKS // BANKS
LAST_GROUPS = (2, 3)
PIECES = ((0, 1), (1, 5), (5, 9))
PADDED = W + 2
IMAGE = H * W
EPS = 1e-5
TAP_SCALE = 64.0
VARIANTS = 2 * TAPS
TAP_COLS = -(-PARTS // TAPS) * TAPS
MATRIX = 132
SETS = TAPS * TAPS
BY_VECTOR, BY_POOL = (0, 1, 3), (2,)
XBUFS = 4
LAPS = (B - XBUFS) // XBUFS

INPUTS = TAPS * C + TAPS
LOADS = BLOCKS
STORES = BLOCKS + 2

_AT = {}
_N = 0
for _name, _width in (("average", PARTS), ("band", TAP_COLS), ("centre", GROUPS * SETS), ("spread", INPUTS),
                      ("phase", PARTS), ("own", SLOTS), ("counts", GROUPS * 2 * 6)):
    _AT[_name] = (_N, _N + _width)
    _N += _width
CONST_COLS = _N


def place():
    p = np.arange(PARTS)
    return p % SLOTS, p // SLOTS


def constants():
    slot, row = place()
    own = slot[:, None] == np.arange(SLOTS)[None, :]
    same = slot[:, None] == slot[None, :]
    near = np.abs(row[:, None] - row[None, :]) <= 1
    phase = np.arange(PARTS) % TAPS
    c = np.zeros((PARTS, CONST_COLS), np.float32)

    def put(name, value):
        a, b = _AT[name]
        c[:value.shape[0], a:b] = value.reshape(value.shape[0], -1)

    new = np.where(row < ROWS - STEP, W, SPAN).astype(np.float32) / np.float32(IMAGE)
    put("average", same * new[:, None])
    counts = np.ones((PARTS, GROUPS, 2, 6), np.float32)
    counts[row < ROWS - STEP] = 0.0
    put("counts", counts)
    band = np.zeros((PARTS, TAP_COLS), np.float32)
    band[:, :PARTS] = same & near
    put("band", band)
    centre = np.zeros((PARTS, GROUPS, TAPS, TAPS), np.float32)
    for p in range(PARTS):
        centre[p, :, 1, phase[p]] = -1.0
    put("centre", centre)
    spread = np.zeros((PARTS, INPUTS), np.float32)
    spread[:, :TAPS * C] = np.tile(np.repeat(own & (row == 0)[:, None], GROUPS, axis=1), (1, TAPS))
    spread[0, TAPS * C:] = 1.0
    put("spread", spread)
    of = np.concatenate([np.repeat(np.arange(TAPS), C), np.arange(TAPS)])
    put("phase", of[:, None] == phase[None, :])
    put("own", own.astype(np.float32))
    return c


def lay_out(w1, b1, fscale, conv_bias):
    slot, _ = place()
    w = w1.reshape(SLOTS, GROUPS, TAPS, TAPS, SLOTS, GROUPS)
    b = b1.reshape(SLOTS, GROUPS, TAPS, TAPS)
    wr = np.zeros((TAPS, SLOTS, GROUPS, GROUPS, TAPS, TAPS, SLOTS), np.float32)
    br = np.zeros((TAPS, GROUPS, TAPS, TAPS, SLOTS), np.float32)
    for q in range(TAPS):
        for ph in range(TAPS):
            tap = (q - ph + 1) % TAPS
            wr[ph, :, :, :, :, q, :] = w[:, :, tap].transpose(3, 4, 1, 2, 0)
            br[ph, :, :, q, :] = b[:, :, tap].transpose(1, 2, 0)
    wr = np.concatenate([wr.reshape(TAPS * C, -1), br.reshape(TAPS, -1)])
    gate = np.stack([fscale.reshape(SLOTS, GROUPS)[slot], conv_bias.reshape(SLOTS, GROUPS)[slot]], axis=1)
    return wr, np.ascontiguousarray(gate.reshape(PARTS, -1))


def build(nc, x, w1r, gate, const, out):
    with ExitStack() as ctx:
        def sb(name, shape, dt=F32):
            return ctx.enter_context(nc.sbuf_tensor(name, shape, dt))

        def ps(name, shape):
            return ctx.enter_context(nc.psum_tensor(name, shape, F32))

        def sem(name):
            return ctx.enter_context(nc.semaphore(name))

        cst = sb("cst", [PARTS, CONST_COLS])
        w1s = sb("w1s", [INPUTS, GROUPS * SETS * SLOTS])
        gates = sb("gates", [PARTS, 2, GROUPS])
        band = sb("band", [PARTS, TAP_COLS], F16)
        ones = sb("ones", [PARTS, PARTS])
        numbers = sb("numbers", [PARTS, 4, GROUPS])
        minus_half, eps, inv_scale, tap_scale = (numbers[:, k] for k in range(4))
        neg_fs = sb("neg_fs", [PARTS, GROUPS])
        bias64 = sb("bias64", [PARTS, GROUPS])

        def const_of(name, parts=PARTS):
            a, b = _AT[name]
            return cst[0:parts, a:b]

        xs = sb("xs", [PARTS, XBUFS, GROUPS, SPAN])
        z_hi = sb("z_hi", [PARTS, 2, GROUPS, BLOCKS, PADDED], F16)
        z_lo = sb("z_lo", [PARTS, 2, GROUPS, BLOCKS, PADDED], F16)
        taps = sb("taps", [PARTS, 2, GROUPS, VARIANTS, MATRIX], F16)
        z_last = sb("z_last", [PARTS, SPAN])
        outs = sb("outs", [PARTS, 2, GROUPS, SPAN])
        gated = sb("gated", [PARTS, GROUPS, SPAN])

        pieces = sb("pieces", [PARTS, GROUPS, len(PIECES), 6])
        row_stats = sb("row_stats", [PARTS, GROUPS, 2])
        neg_mean = sb("neg_mean", [PARTS, 2, GROUPS])
        moments = sb("moments", [PARTS, 2, GROUPS])
        square = sb("square", [PARTS, GROUPS])
        zstats = sb("zstats", [PARTS, 2, GROUPS])
        var_eps = sb("var_eps", [PARTS, GROUPS])
        rstd = sb("rstd", [PARTS, XBUFS, GROUPS])
        rstd64 = sb("rstd64", [PARTS, GROUPS])
        gate_scale = sb("gate_scale", [PARTS, XBUFS, GROUPS])
        gate_part = sb("gate_part", [PARTS, GROUPS])
        gate_bias = sb("gate_bias", [PARTS, XBUFS, GROUPS])
        skip_scale = sb("skip_scale", [PARTS, XBUFS, GROUPS])
        skip_bias = sb("skip_bias", [PARTS, XBUFS, GROUPS])
        avg = sb("avg", [PARTS, GROUPS])
        avg_cols = sb("avg_cols", [PARTS, INPUTS])
        avg_rows = sb("avg_rows", [INPUTS, PARTS])
        own_dyn = sb("own_dyn", [PARTS, GROUPS * SETS, SLOTS])
        dyn = sb("dyn", [PARTS, GROUPS * SETS])
        sig = sb("sig", [PARTS, GROUPS * SETS])
        less_one = sb("less_one", [PARTS, GROUPS * SETS])
        tap = sb("tap", [PARTS, GROUPS, SETS])
        tap_split = sb("tap_split", [PARTS, 2, GROUPS, 2, SETS], F16)

        conv_ps = ps("conv_ps", [128, 2, BANKS, 512])
        stat_ps = ps("stat_ps", [128, 512])
        dyn_ps = ps("dyn_ps", [128, 512])
        mean_ps = stat_ps[:, 0:GROUPS]
        zstats_ps = stat_ps[:, GROUPS:3 * GROUPS]
        avg_ps = stat_ps[0:INPUTS, 128:128 + PARTS]

        first_loaded = [sem(f"first_loaded{i}") for i in range(len(PIECES))]
        x_loaded = [sem(f"x_loaded{i}") for i in range(XBUFS)]
        outs_free = [sem(f"outs_free{i}") for i in range(2)]
        params_loaded = sem("params_loaded")
        consts_loaded = sem("consts_loaded")
        pads_zeroed = sem("pads_zeroed")
        table_loaded = sem("table_loaded")
        ones_set = sem("ones_set")
        gate_params_set = sem("gate_params_set")
        band_set = sem("band_set")
        last_columns_set = sem("last_columns_set")
        pieces_done = sem("pieces_done")
        counted_ready = sem("counted_ready")
        rows_done = sem("rows_done")
        mean_done = sem("mean_done")
        neg_mean_ready = sem("neg_mean_ready")
        dev_ready = sem("dev_ready")
        square_ready = sem("square_ready")
        moments_ready = sem("moments_ready")
        zstats_done = sem("zstats_done")
        zstats_copied = sem("zstats_copied")
        var_eps_ready = sem("var_eps_ready")
        rstd_ready = sem("rstd_ready")
        avg_ready = sem("avg_ready")
        avg_cols_ready = sem("avg_cols_ready")
        gate_scale_ready = sem("gate_scale_ready")
        gate_part_ready = sem("gate_part_ready")
        affine_ready = sem("affine_ready")
        avg_rows_done = sem("avg_rows_done")
        avg_rows_ready = sem("avg_rows_ready")
        dyn_done = sem("dyn_done")
        own_dyn_ready = sem("own_dyn_ready")
        dyn_ready = sem("dyn_ready")
        sig_ready = sem("sig_ready")
        less_one_ready = sem("less_one_ready")
        tap_ready = sem("tap_ready")
        tap_hi_ready = sem("tap_hi_ready")
        tap_split_ready = sem("tap_split_ready")
        vector_taps_ready, pool_taps_ready = sem("vector_taps_ready"), sem("pool_taps_ready")
        z_hi_ready = sem("z_hi_ready")
        z_lo_ready = sem("z_lo_ready")
        z_last_ready = sem("z_last_ready")
        last_z_lo_ready = sem("last_z_lo_ready")
        conv_done = sem("conv_done")
        gate_ready = sem("gate_ready")
        skip_ready = sem("skip_ready")
        gated_ready = sem("gated_ready")
        out_ready = sem("out_ready")
        bank_done = sem("bank_done")
        bank_gated = sem("bank_gated")
        out_bank_ready = sem("out_bank_ready")

        block = ctx.enter_context(nc.Block())

        def at_least(eng, s, value):
            if not isinstance(value, int) or value > 0:
                eng.wait_ge(s, value)

        def batch(lap, v):
            return XBUFS * lap + 1 + v

        def uses(lap, v):
            return lap + (1 + v) // XBUFS + (1 if (1 + v) % XBUFS else 0)

        def in_batches(v_and_after, lap):
            return not isinstance(lap, int) or 0 <= XBUFS * lap + 1 + v_and_after < B

        def is_last(lap, v):
            return isinstance(lap, int) and batch(lap, v) == B - 1

        def schedule(eng, step):
            with eng.Fori(0, LAPS) as lap:
                for v in range(XBUFS):
                    step(lap, v)
            for v in range(B - 1 - XBUFS * LAPS):
                step(LAPS, v)

        def matrices(eng, lap, v, g):
            i, par = batch(lap, v), (1 + v) % 2
            eng.wait_ge(tap_split_ready, i + 1)
            shape = [PARTS, VARIANTS, TAP_COLS // TAPS, TAPS]
            eng.tensor_tensor(
                taps[:, par, g, :, 0:TAP_COLS].rearrange("p t (a q) -> p t a q", q=TAPS),
                band[:].rearrange("p (a q) -> p a q", q=TAPS).unsqueeze(1).to_broadcast(shape),
                tap_split[:, par, g].rearrange("p h (d q) -> p (h d) q", q=TAPS).unsqueeze(2).to_broadcast(shape),
                ALU.mult).then_inc(pool_taps_ready if g in BY_POOL else vector_taps_ready, 1)

        @block.sync
        def _(sp):

            def rows_of(image, first, count):
                return bass.AP(image.tensor, image.offset + first * W, [[W, count], [IMAGE, C], [1, W]])

            def load(lap, v):
                i, buf = batch(lap, v), (1 + v) % XBUFS
                if not isinstance(i, int) or i >= XBUFS:
                    sp.wait_ge(skip_ready, GROUPS * i - GROUPS * (XBUFS - 1))
                    sp.wait_ge(z_lo_ready, (GROUPS - 1) * i - (GROUPS - 1) * (XBUFS - 1))
                src = x[i]
                for k in range(BLOCKS):
                    sp.dma_start(xs[:, buf, :, k * W:(k + 1) * W], rows_of(src, STEP * k, ROWS)).then_inc(x_loaded[buf], 16)

            def load_first():
                for k in range(BLOCKS):
                    piece = [a <= k < b for a, b in PIECES].index(True)
                    sp.dma_start(xs[:, 0, :, k * W:(k + 1) * W], rows_of(x[0], STEP * k, ROWS)).then_inc(first_loaded[piece], 16)

            def store_blocks(i, par, blocks):
                for k in blocks:
                    sp.dma_start(rows_of(out[i], STEP * k + 1, STEP),
                                 outs[SLOTS:PARTS - SLOTS, par, :, k * W:(k + 1) * W]).then_inc(outs_free[par], 16)
                    if k == 0:
                        sp.dma_start(rows_of(out[i], 0, 1), outs[0:SLOTS, par, :, 0:W]).then_inc(outs_free[par], 16)
                    if k == BLOCKS - 1:
                        sp.dma_start(rows_of(out[i], H - 1, 1), outs[PARTS - SLOTS:, par, :, SPAN - W:]).then_inc(outs_free[par], 16)

            def store(lap, v):
                sp.wait_ge(out_ready, GROUPS * batch(lap, v) + GROUPS)
                store_blocks(batch(lap, v), (1 + v) % 2, range(BLOCKS))

            def store_last():
                sp.wait_ge(out_ready, GROUPS * B - len(LAST_GROUPS))
                for bank in range(BANKS):
                    sp.wait_ge(out_bank_ready, len(LAST_GROUPS) * (bank + 1))
                    store_blocks(B - 1, (B - 1) % 2, range(PER_BANK * bank, PER_BANK * (bank + 1)))

            def step(lap, v):
                if in_batches(v + 3, lap):
                    load(lap, v + 3)
                store(lap, v - 1)

            load_first()
            sp.dma_start(cst[:], const).then_inc(consts_loaded, 16)
            sp.dma_start(w1s[:], w1r).then_inc(params_loaded, 16)
            sp.dma_start(gates[:].rearrange("p a g -> p (a g)"), gate).then_inc(params_loaded, 16)
            for v in range(XBUFS - 1):
                load(0, v)
            schedule(sp, step)
            store_last()
            for par in range(2):
                sp.wait_ge(outs_free[par], 16 + 16 * STORES * (B // 2))

        @block.tensor
        def _(pe):
            pe.wait_ge(consts_loaded, 16)
            pe.wait_ge(ones_set, 5)

            def mean(lap, v):
                i = batch(lap, v)
                pe.wait_ge(rows_done, i + 1)
                nc.tensor.matmul(mean_ps, const_of("average"), row_stats[:, :, 0],
                                 start=True, stop=True).then_inc(mean_done, 1)

            def spread_stats(lap, v):
                i = batch(lap, v)
                pe.wait_ge(moments_ready, i + 1)
                nc.tensor.matmul(zstats_ps, const_of("average"),
                                 moments[:].rearrange("p a g -> p (a g)"), start=True, stop=True).then_inc(zstats_done, 1)

            def averages(lap, v):
                i = batch(lap, v)
                pe.wait_ge(avg_cols_ready, i + 1)
                nc.tensor.matmul(avg_ps, avg_cols[:], ones[:],
                                 start=True, stop=True).then_inc(avg_rows_done, 1)

            def dynamics(lap, v):
                i = batch(lap, v)
                pe.wait_ge(avg_rows_ready, i + 1)
                nc.tensor.matmul(dyn_ps[0:PARTS, 0:GROUPS * SETS * SLOTS], avg_rows[:], w1s[:],
                                 start=True, stop=True).then_inc(dyn_done, 1)

            def wait_for_group(lap, v, g):
                i = batch(lap, v)
                n = GROUPS * i + g
                at_least(pe, gated_ready, n - 1)
                if g in BY_POOL:
                    pe.wait_ge(pool_taps_ready, len(BY_POOL) * i + BY_POOL.index(g) + 1)
                else:
                    pe.wait_ge(vector_taps_ready, len(BY_VECTOR) * i + BY_VECTOR.index(g) + 1)
                pe.wait_ge(z_hi_ready, n + 1)
                if g < GROUPS - 1:
                    pe.wait_ge(z_lo_ready, (GROUPS - 1) * i + g + 1)
                else:
                    pe.wait_ge(last_z_lo_ready, i + 1)

            products = [(half, z, dw) for half, z in ((0, z_hi), (0, z_lo), (1, z_hi)) for dw in range(TAPS)]

            def product(v, g, at, bank):
                par = (1 + v) % 2
                half, z, dw = products[at]
                return nc.tensor.matmul(conv_ps[:, g % 2, bank, 0:PER_BANK * W], taps[:, par, g, half * TAPS + dw, 0:PARTS],
                                        z[:, par, g, PER_BANK * bank:PER_BANK * (bank + 1), dw:dw + W],
                                        start=at == 0, stop=at == len(products) - 1)

            def conv(lap, v, g):
                wait_for_group(lap, v, g)
                for at in range(len(products)):
                    for bank in range(BANKS):
                        mm = product(v, g, at, bank)
                mm.then_inc(conv_done, 1)

            def conv_by_bank(lap, v):
                for bank in range(BANKS):
                    for g in LAST_GROUPS:
                        if bank == 0:
                            wait_for_group(lap, v, g)
                        for at in range(len(products)):
                            mm = product(v, g, at, bank)
                        mm.then_inc(bank_done, 1)

            def keep_warm(count):
                for _ in range(count):
                    nc.tensor.matmul(conv_ps[:, 1, 0, 0:PARTS], band[:, 0:PARTS], band[:, 0:PARTS], start=True, stop=True)

            def start():
                mean(0, -1)
                spread_stats(0, -1)
                pe.wait_ge(band_set, 1)
                keep_warm(24)
                pe.wait_ge(last_columns_set, 1)
                averages(0, -1)
                pe.wait_ge(params_loaded, 32)
                dynamics(0, -1)
                keep_warm(24)
                conv(0, -1, 0)
                mean(0, 0)
                spread_stats(0, 0)
                conv(0, -1, 1)
                averages(0, 0)
                conv(0, -1, 2)
                dynamics(0, 0)
                mean(0, 1)
                spread_stats(0, 1)
                conv(0, -1, 3)

            def step(lap, v):
                nxt, stats = in_batches(v + 1, lap), in_batches(v + 2, lap)
                if nxt:
                    averages(lap, v + 1)
                conv(lap, v, 0)
                if nxt:
                    dynamics(lap, v + 1)
                if stats:
                    mean(lap, v + 2)
                conv(lap, v, 1)
                if stats:
                    spread_stats(lap, v + 2)
                if is_last(lap, v):
                    conv_by_bank(lap, v)
                else:
                    conv(lap, v, 2)
                    conv(lap, v, 3)

            start()
            schedule(pe, step)

        @block.vector
        def _(dve):
            def bn(lap, v, g):
                buf = (1 + v) % XBUFS
                if g == 0:
                    dve.wait_ge(x_loaded[buf], 16 * LOADS * uses(lap, v))
                for h, (a, b) in enumerate(PIECES):
                    ins = nc.vector.bn_stats(pieces[:, g, h, :], xs[:, buf, g, a * W:b * W])
                ins.then_inc(pieces_done, 1)

            def bn_first():
                for h, (a, b) in enumerate(PIECES):
                    dve.wait_ge(first_loaded[h], 16 * (b - a))
                    for g in range(GROUPS):
                        ins = nc.vector.bn_stats(pieces[:, g, h, :], xs[:, 0, g, a * W:b * W])
                        if h == len(PIECES) - 1:
                            ins.then_inc(pieces_done, 1)

            def count(lap, v):
                dve.wait_ge(pieces_done, GROUPS * (batch(lap, v) + 1))
                nc.vector.tensor_tensor(pieces[:, :, 1:], pieces[:, :, 1:],
                                        const_of("counts").rearrange("p (g k e) -> p g k e", g=GROUPS, e=6),
                                        ALU.mult).then_inc(counted_ready, 1)

            def rows(lap, v):
                for g in range(GROUPS):
                    ins = nc.vector.bn_aggr(row_stats[:, g, :], pieces[:, g].rearrange("p h s -> p (h s)"))
                ins.then_inc(rows_done, 1)

            def channel_mean(lap, v):
                i, par = batch(lap, v), (1 + v) % 2
                dve.wait_ge(mean_done, i + 1)
                nc.vector.tensor_scalar(neg_mean[:, par], mean_ps, -1.0, None, ALU.mult).then_inc(neg_mean_ready, 1)

            def deviations(lap, v):
                i, par = batch(lap, v), (1 + v) % 2
                dve.wait_ge(neg_mean_ready, i + 1)
                nc.vector.tensor_tensor(moments[:, 0], row_stats[:, :, 0], neg_mean[:, par],
                                        ALU.add).then_inc(dev_ready, 1)

            def squares(lap, v):
                i = batch(lap, v)
                dve.wait_ge(dev_ready, i + 1)
                nc.vector.tensor_tensor(square[:], moments[:, 0], moments[:, 0], ALU.mult).then_inc(square_ready, 1)
                dve.wait_ge(square_ready, i + 1)
                nc.vector.tensor_tensor(moments[:, 1], row_stats[:, :, 1], square[:], ALU.add).then_inc(moments_ready, 1)

            def copy_stats(lap, v):
                dve.wait_ge(zstats_done, batch(lap, v) + 1)
                nc.vector.tensor_copy(zstats[:].rearrange("p a g -> p (a g)"), zstats_ps).then_inc(zstats_copied, 1)

            def channel_averages(lap, v):
                i, buf = batch(lap, v), (1 + v) % XBUFS
                dve.wait_ge(rstd_ready, i + 1)
                nc.vector.tensor_tensor(avg[:], zstats[:, 0], rstd[:, buf], ALU.mult).then_inc(avg_ready, 1)

            def average_columns(lap, v):
                dve.wait_ge(avg_ready, batch(lap, v) + 1)
                nc.vector.tensor_tensor(avg_cols[:, 0:TAPS * C].rearrange("p (a g) -> p a g", g=GROUPS),
                                        const_of("spread")[:, 0:TAPS * C].rearrange("p (a g) -> p a g", g=GROUPS),
                                        avg[:].unsqueeze(1).to_broadcast([PARTS, TAPS * SLOTS, GROUPS]),
                                        ALU.mult).then_inc(avg_cols_ready, 1)

            def avg_of_phase(lap, v):
                i = batch(lap, v)
                dve.wait_ge(avg_rows_done, i + 1)
                nc.vector.tensor_tensor(avg_rows[:], avg_ps, const_of("phase", INPUTS),
                                        ALU.mult).then_inc(avg_rows_ready, 1)

            def own_products(lap, v):
                i = batch(lap, v)
                dve.wait_ge(dyn_done, i + 1)
                nc.vector.tensor_tensor(own_dyn[:], dyn_ps[0:PARTS, 0:GROUPS * SETS * SLOTS].rearrange("p (a c) -> p a c", c=SLOTS),
                                        const_of("own").unsqueeze(1).to_broadcast([PARTS, GROUPS * SETS, SLOTS]),
                                        ALU.mult).then_inc(own_dyn_ready, 1)

            def own_taps(lap, v):
                i = batch(lap, v)
                dve.wait_ge(own_dyn_ready, i + 1)
                nc.vector.tensor_reduce(dyn[:], own_dyn[:], AX_X, ALU.add).then_inc(dyn_ready, 1)

            def low(lap, v, g):
                i, par, buf = batch(lap, v), (1 + v) % 2, (1 + v) % XBUFS
                n = GROUPS * i + g
                at_least(dve, conv_done, n + 1 - 2 * GROUPS)
                dve.wait_ge(z_hi_ready, n + 1)
                nc.vector.scalar_tensor_tensor(
                    out=z_lo[:, par, g, :, 1:W + 1], in0=xs[:, buf, g].rearrange("p (k w) -> p k w", w=W),
                    scalar=neg_mean[:, par, g:g + 1], in1=z_hi[:, par, g, :, 1:W + 1],
                    op0=ALU.add, op1=ALU.subtract).then_inc(z_lo_ready, 1)

            def gate_conv(lap, v, g):
                n = GROUPS * batch(lap, v) + g
                dve.wait_ge(gate_ready, n + 1)
                dve.wait_ge(conv_done, n + 1)
                tile = gated[:, g].rearrange("p (h n) -> p h n", h=BANKS)
                nc.vector.scalar_tensor_tensor(out=tile, in0=conv_ps[:, g % 2, :, 0:PER_BANK * W], scalar=bias64[:, g:g + 1],
                                               in1=tile, op0=ALU.add, op1=ALU.mult).then_inc(gated_ready, 1)

            def gate_conv_by_bank():
                par = (B - 1) % 2
                dve.wait_ge(gate_ready, GROUPS * B)
                dve.wait_ge(skip_ready, GROUPS * B)
                for bank in range(BANKS):
                    columns = slice(bank * PER_BANK * W, (bank + 1) * PER_BANK * W)
                    done = len(LAST_GROUPS) * bank
                    for k, g in enumerate(LAST_GROUPS):
                        dve.wait_ge(bank_done, done + k + 1)
                        nc.vector.scalar_tensor_tensor(out=gated[:, g, columns], in0=conv_ps[:, g % 2, bank, 0:PER_BANK * W],
                                                       scalar=bias64[:, g:g + 1], in1=gated[:, g, columns],
                                                       op0=ALU.add, op1=ALU.mult).then_inc(bank_gated, 1)
                    for k, g in enumerate(LAST_GROUPS):
                        dve.wait_ge(bank_gated, done + k + 1)
                        nc.vector.tensor_tensor(outs[:, par, g, columns], outs[:, par, g, columns], gated[:, g, columns],
                                                ALU.add).then_inc(out_bank_ready, 1)

            def start():
                bn_first()
                dve.wait_ge(consts_loaded, 16)
                count(0, -1)
                dve.wait_ge(counted_ready, 1)
                rows(0, -1)
                nc.vector.tensor_copy(band[:], const_of("band")).then_inc(band_set, 1)
                nc.vector.tensor_copy(avg_cols[:, TAPS * C:], const_of("spread")[:, TAPS * C:]).then_inc(last_columns_set, 1)
                channel_mean(0, -1)
                deviations(0, -1)
                squares(0, -1)
                dve.wait_ge(pads_zeroed, 4)
                low(0, -1, 0)
                copy_stats(0, -1)
                low(0, -1, 1)
                channel_averages(0, -1)
                average_columns(0, -1)
                bn(0, 0, 0)
                avg_of_phase(0, -1)
                low(0, -1, 2)
                own_products(0, -1)
                own_taps(0, -1)
                bn(0, 0, 1)
                matrices(nc.vector, 0, -1, 0)
                matrices(nc.vector, 0, -1, 1)
                bn(0, 0, 2)
                bn(0, 0, 3)
                count(0, 0)
                dve.wait_ge(counted_ready, 2)
                rows(0, 0)
                channel_mean(0, 0)
                deviations(0, 0)
                squares(0, 0)
                dve.wait_ge(gate_params_set, 2)
                gate_conv(0, -1, 0)
                copy_stats(0, 0)
                bn(0, 1, 0)
                channel_averages(0, 0)
                bn(0, 1, 1)
                average_columns(0, 0)
                matrices(nc.vector, 0, -1, 3)
                bn(0, 1, 2)
                gate_conv(0, -1, 1)
                bn(0, 1, 3)
                avg_of_phase(0, 0)
                count(0, 1)
                low(0, 0, 0)
                dve.wait_ge(counted_ready, 3)
                rows(0, 1)
                own_products(0, 0)
                channel_mean(0, 1)
                own_taps(0, 0)
                deviations(0, 1)
                squares(0, 1)
                gate_conv(0, -1, 2)
                copy_stats(0, 1)
                low(0, 0, 1)
                matrices(nc.vector, 0, 0, 0)
                channel_averages(0, 1)
                matrices(nc.vector, 0, 0, 1)
                average_columns(0, 1)
                bn(0, 2, 0)
                bn(0, 2, 1)
                gate_conv(0, -1, 3)
                avg_of_phase(0, 1)
                bn(0, 2, 2)
                bn(0, 2, 3)
                count(0, 2)
                dve.wait_ge(counted_ready, 4)
                rows(0, 2)
                low(0, 0, 2)
                dve.wait_ge(z_lo_ready, 2 * (GROUPS - 1))

            def step(lap, v):
                nxt, stats, rows_in = (in_batches(v + k, lap) for k in (1, 2, 3))
                if nxt:
                    low(lap, v + 1, 0)
                    low(lap, v + 1, 1)
                gate_conv(lap, v, 0)
                if stats:
                    channel_mean(lap, v + 2)
                if nxt:
                    own_products(lap, v + 1)
                if stats:
                    deviations(lap, v + 2)
                if nxt:
                    own_taps(lap, v + 1)
                if stats:
                    squares(lap, v + 2)
                if nxt:
                    low(lap, v + 1, 2)
                gate_conv(lap, v, 1)
                if stats:
                    copy_stats(lap, v + 2)
                matrices(nc.vector, lap, v, 3)
                if rows_in:
                    bn(lap, v + 3, 0)
                    bn(lap, v + 3, 1)
                if not is_last(lap, v):
                    gate_conv(lap, v, 2)
                if stats:
                    channel_averages(lap, v + 2)
                if nxt:
                    matrices(nc.vector, lap, v + 1, 0)
                if stats:
                    average_columns(lap, v + 2)
                if nxt:
                    matrices(nc.vector, lap, v + 1, 1)
                if rows_in:
                    bn(lap, v + 3, 2)
                if rows_in:
                    bn(lap, v + 3, 3)
                if stats:
                    avg_of_phase(lap, v + 2)
                if rows_in:
                    count(lap, v + 3)
                if rows_in:
                    dve.wait_ge(counted_ready, batch(lap, v + 3) + 1)
                if is_last(lap, v):
                    gate_conv_by_bank()
                else:
                    gate_conv(lap, v, 3)
                if rows_in:
                    rows(lap, v + 3)

            start()
            schedule(dve, step)

        @block.scalar
        def _(act):
            act.wait_ge(ones_set, 5)
            nc.scalar.activation(sig[:, 0:1], ones[:, 0:1], ACT.Sigmoid).then_inc(table_loaded, 1)
            act.wait_ge(table_loaded, 1)
            act.wait_ge(pads_zeroed, 4)

            def high(lap, v, g):
                i, par, buf = batch(lap, v), (1 + v) % 2, (1 + v) % XBUFS
                n = GROUPS * i + g
                if g == 0:
                    act.wait_ge(neg_mean_ready, i + 1)
                at_least(act, conv_done, n + 1 - 2 * GROUPS)
                nc.scalar.activation(z_hi[:, par, g, :, 1:W + 1], xs[:, buf, g].rearrange("p (k w) -> p k w", w=W),
                                     ACT.Identity, bias=neg_mean[:, par, g:g + 1]).then_inc(z_hi_ready, 1)

            def last_z(lap, v):
                i, par, buf = batch(lap, v), (1 + v) % 2, (1 + v) % XBUFS
                at_least(act, last_z_lo_ready, i)
                nc.scalar.activation(z_last[:], xs[:, buf, GROUPS - 1], ACT.Identity,
                                     bias=neg_mean[:, par, GROUPS - 1:]).then_inc(z_last_ready, 1)

            def gate_and_skip(lap, v, g):
                i, par, buf = batch(lap, v), (1 + v) % 2, (1 + v) % XBUFS
                n = GROUPS * i + g
                if g == 0:
                    act.wait_ge(affine_ready, 3 * (i + 1))
                at_least(act, out_ready, n + 1 - GROUPS)
                nc.scalar.activation(gated[:, g], xs[:, buf, g], ACT.Identity, bias=gate_bias[:, buf, g:g + 1],
                                     scale=gate_scale[:, buf, g:g + 1]).then_inc(gate_ready, 1)
                if g == 0:
                    act.wait_ge(outs_free[par], 16 + 16 * STORES * (XBUFS // 2 * lap + (1 + v) // 2))
                nc.scalar.activation(outs[:, par, g], xs[:, buf, g], ACT.Identity, bias=skip_bias[:, buf, g:g + 1],
                                     scale=skip_scale[:, buf, g:g + 1]).then_inc(skip_ready, 1)

            def sigmoid(lap, v):
                act.wait_ge(dyn_ready, batch(lap, v) + 1)
                nc.scalar.activation(sig[:], dyn[:], ACT.Sigmoid).then_inc(sig_ready, 1)

            def step(lap, v):
                nxt = in_batches(v + 1, lap)
                for s in range(GROUPS):
                    if nxt:
                        high(lap, v + 1, s)
                    if nxt and s == 3:
                        last_z(lap, v + 1)
                    gate_and_skip(lap, v, s)
                    if nxt and s == 2:
                        sigmoid(lap, v + 1)

            for g in range(GROUPS - 1):
                high(0, -1, g)
            sigmoid(0, -1)
            high(0, -1, GROUPS - 1)
            last_z(0, -1)
            gate_and_skip(0, -1, 0)
            high(0, 0, 0)
            gate_and_skip(0, -1, 1)
            high(0, 0, 1)
            gate_and_skip(0, -1, 2)
            high(0, 0, 2)
            high(0, 0, 3)
            sigmoid(0, 0)
            last_z(0, 0)
            gate_and_skip(0, -1, 3)
            schedule(act, step)

        @block.gpsimd
        def _(pool):
            for par in range(2):
                for z in (z_hi, z_lo):
                    nc.gpsimd.memset(z[:, par, :, :, 0:PADDED:W + 1].rearrange("p g k e -> p (g k) e"), 0.0).then_inc(pads_zeroed, 1)
            for par in range(2):
                nc.gpsimd.memset(outs[:, par, 0, 0:1], 0.0).then_inc(outs_free[par], 16)
            nc.gpsimd.memset(ones[:], 1.0).then_inc(ones_set, 1)
            for tile, number in ((minus_half, -0.5), (eps, EPS), (inv_scale, 1.0 / TAP_SCALE), (tap_scale, TAP_SCALE)):
                nc.gpsimd.memset(tile, number).then_inc(ones_set, 1)
            pool.wait_ge(params_loaded, 32)
            nc.gpsimd.tensor_scalar(neg_fs[:], gates[:, 0], -1.0 / TAP_SCALE, 0.0, ALU.mult, ALU.add).then_inc(gate_params_set, 1)
            nc.gpsimd.tensor_scalar(bias64[:], gates[:, 1], TAP_SCALE, 0.0, ALU.mult, ALU.add).then_inc(gate_params_set, 1)
            pool.wait_ge(consts_loaded, 16)
            pool.wait_ge(ones_set, 5)
            pool.wait_ge(gate_params_set, 2)
            pool.wait_ge(band_set, 1)

            def inverse_deviation(lap, v):
                i, buf = batch(lap, v), (1 + v) % XBUFS
                pool.wait_ge(zstats_copied, i + 1)
                nc.gpsimd.tensor_tensor(var_eps[:], zstats[:, 1], eps, ALU.add).then_inc(var_eps_ready, 1)
                pool.wait_ge(var_eps_ready, i + 1)
                nc.gpsimd.tensor_tensor(rstd[:, buf], var_eps[:], minus_half, ALU.pow).then_inc(rstd_ready, 1)

            def factors(lap, v):
                i, par, buf = batch(lap, v), (1 + v) % 2, (1 + v) % XBUFS
                pool.wait_ge(rstd_ready, i + 1)
                nc.gpsimd.tensor_tensor(gate_scale[:, buf], neg_fs[:], rstd[:, buf], ALU.mult).then_inc(gate_scale_ready, 1)
                nc.gpsimd.tensor_tensor(skip_bias[:, buf], rstd[:, buf], neg_mean[:, par], ALU.mult).then_inc(affine_ready, 1)
                nc.gpsimd.tensor_tensor(skip_scale[:, buf], rstd[:, buf], ones[:, 0:GROUPS], ALU.add).then_inc(affine_ready, 1)
                pool.wait_ge(gate_scale_ready, i + 1)
                nc.gpsimd.tensor_tensor(gate_part[:], gate_scale[:, buf], neg_mean[:, par], ALU.mult).then_inc(gate_part_ready, 1)
                pool.wait_ge(gate_part_ready, i + 1)
                nc.gpsimd.tensor_tensor(gate_bias[:, buf], gate_part[:], inv_scale, ALU.add).then_inc(affine_ready, 1)

            def split_taps(lap, v):
                i, par, buf = batch(lap, v), (1 + v) % 2, (1 + v) % XBUFS
                pool.wait_ge(rstd_ready, i + 1)
                nc.gpsimd.tensor_tensor(rstd64[:], rstd[:, buf], tap_scale, ALU.mult).then_inc(less_one_ready, 1)
                pool.wait_ge(sig_ready, i + 1)
                nc.gpsimd.tensor_tensor(less_one[:], sig[:], const_of("centre"), ALU.add).then_inc(less_one_ready, 1)
                pool.wait_ge(less_one_ready, 2 * (i + 1))
                nc.gpsimd.tensor_tensor(tap[:], less_one[:].rearrange("p (g t) -> p g t", g=GROUPS),
                                        rstd64[:].unsqueeze(2).to_broadcast([PARTS, GROUPS, SETS]), ALU.mult).then_inc(tap_ready, 1)
                pool.wait_ge(tap_ready, i + 1)
                nc.gpsimd.tensor_tensor(tap_split[:, par, :, 0, :], tap[:], ones[:, 0:GROUPS * SETS].rearrange("p (g t) -> p g t", g=GROUPS),
                                        ALU.mult).then_inc(tap_hi_ready, 1)
                pool.wait_ge(tap_hi_ready, i + 1)
                nc.gpsimd.tensor_tensor(tap_split[:, par, :, 1, :], tap[:], tap_split[:, par, :, 0, :],
                                        ALU.subtract).then_inc(tap_split_ready, 1)

            def last_low(lap, v):
                i, par = batch(lap, v), (1 + v) % 2
                at_least(pool, conv_done, GROUPS * i - GROUPS)
                pool.wait_ge(z_last_ready, i + 1)
                nc.gpsimd.tensor_tensor(z_lo[:, par, GROUPS - 1, :, 1:W + 1], z_last[:].rearrange("p (k w) -> p k w", w=W),
                                        z_hi[:, par, GROUPS - 1, :, 1:W + 1], ALU.subtract).then_inc(last_z_lo_ready, 1)

            def add_skip(lap, v, g):
                par, n = (1 + v) % 2, GROUPS * batch(lap, v) + g
                pool.wait_ge(skip_ready, n + 1)
                pool.wait_ge(gated_ready, n + 1)
                nc.gpsimd.tensor_tensor(outs[:, par, g], outs[:, par, g], gated[:, g], ALU.add).then_inc(out_ready, 1)

            def step(lap, v):
                nxt, stats = in_batches(v + 1, lap), in_batches(v + 2, lap)
                matrices(nc.gpsimd, lap, v, BY_POOL[0])
                add_skip(lap, v, 0)
                if nxt:
                    split_taps(lap, v + 1)
                add_skip(lap, v, 1)
                if stats:
                    inverse_deviation(lap, v + 2)
                if not is_last(lap, v):
                    add_skip(lap, v, 2)
                if stats:
                    factors(lap, v + 2)
                if nxt:
                    last_low(lap, v + 1)
                if not is_last(lap, v):
                    add_skip(lap, v, 3)

            inverse_deviation(0, -1)
            factors(0, -1)
            split_taps(0, -1)
            matrices(nc.gpsimd, 0, -1, BY_POOL[0])
            last_low(0, -1)
            inverse_deviation(0, 0)
            factors(0, 0)
            add_skip(0, -1, 0)
            add_skip(0, -1, 1)
            split_taps(0, 0)
            inverse_deviation(0, 1)
            add_skip(0, -1, 2)
            factors(0, 1)
            last_low(0, 0)
            add_skip(0, -1, 3)
            schedule(pool, step)


def kernel(x, L0_conv_w1, L0_conv_b1, L0_conv_fscale, L0_conv_conv_bias):
    from concourse import bacc
    from concourse.bass_utils import run_bass_kernel_spmd

    w1r, gate = lay_out(np.asarray(L0_conv_w1), np.asarray(L0_conv_b1), np.asarray(L0_conv_fscale),
                             np.asarray(L0_conv_conv_bias))
    arrays = {"x": np.ascontiguousarray(x), "w1r": w1r, "gate": gate, "const": constants()}
    nc = bacc.Bacc("TRN2", target_bir_lowering=False, num_devices=1)
    ins = [nc.dram_tensor(n, a.shape, mybir.dt.from_np(a.dtype), kind="ExternalInput").ap() for n, a in arrays.items()]
    out = nc.dram_tensor("out", (B, C, H, W), F32, kind="ExternalOutput").ap()
    build(nc, *ins, out)
    return run_bass_kernel_spmd(nc, [arrays], core_ids=[0]).results[0]["out"]
```
